# Optimizing a Trainium2 kernel written in Bass

```python
import numpy as np
import jax
import jax.numpy as jnp

def _softmax(x, axis=-1):
    return jax.nn.softmax(x, axis=axis)

def _gelu(x):
    return jax.nn.gelu(x, approximate=True)

def _silu(x):
    return jax.nn.silu(x)

def _sigmoid(x):
    return jax.nn.sigmoid(x)

def _layernorm(x, axis=-1, eps=1e-05):
    m = jnp.mean(x, axis=axis, keepdims=True)
    v = jnp.var(x, axis=axis, keepdims=True)
    return (x - m) / jnp.sqrt(v + eps)

def _scatter_add(tgt, idx, src, axis=0):
    return tgt.at[idx].add(src)

def _segment_sum(src, seg, n):
    return jax.ops.segment_sum(src, seg, n)
kernel_name = 'mk_sandwich_d1_jaxref_r4_ddaa05'

def setup_inputs(seed: int=0):
    np.random.seed(seed)
    _w = jnp.asarray

    def _L0_attn_setup():
        import jax, jax.numpy as jnp
        import numpy as np
        import math
        D_MODEL = 512
        N_HEADS = 16
        D_HEAD = 128
        BATCH = 2
        SEQ = 512
        key = jax.random.key(seed)
        ks = jax.random.split(key, 5)
        std = 0.02
        x = jax.random.normal(ks[0], (BATCH, SEQ, D_MODEL), dtype=jnp.float32)
        W_Q = std * jax.random.normal(ks[1], (N_HEADS, D_HEAD, D_MODEL), dtype=jnp.float32)
        W_K = std * jax.random.normal(ks[2], (N_HEADS, D_HEAD, D_MODEL), dtype=jnp.float32)
        W_V = std * jax.random.normal(ks[3], (N_HEADS, D_HEAD, D_MODEL), dtype=jnp.float32)
        W_O = std * jax.random.normal(ks[4], (N_HEADS, D_MODEL, D_HEAD), dtype=jnp.float32)
        return {'x': x, 'W_Q': W_Q, 'W_K': W_K, 'W_V': W_V, 'W_O': W_O}
    _L0_attn_in = _L0_attn_setup()

    def _L0_ffn_setup():
        import jax, jax.numpy as jnp
        import numpy as np
        D_MODEL = 512
        HIDDEN = int(2 * D_MODEL * 4 / 3)

        def ternary_quant(w):
            s = jnp.mean(jnp.abs(w))
            q = jnp.clip(jnp.round(w / s), -1.0, 1.0) * s
            return w + jax.lax.stop_gradient(q - w)
        key = jax.random.key(seed)
        k0, k1, k2, k3 = jax.random.split(key, 4)
        x = jax.random.normal(k0, (4, 1024, D_MODEL), dtype=jnp.float32)
        std_in = 1.0 / np.sqrt(D_MODEL)
        std_h = 1.0 / np.sqrt(HIDDEN)
        w1 = jax.random.uniform(k1, (HIDDEN, D_MODEL), jnp.float32, -std_in, std_in)
        w3 = jax.random.uniform(k2, (HIDDEN, D_MODEL), jnp.float32, -std_in, std_in)
        w2 = jax.random.uniform(k3, (D_MODEL, HIDDEN), jnp.float32, -std_h, std_h)
        return {'x': x, 'w1': w1, 'w3': w3, 'w2': w2}
    _L0_ffn_in = _L0_ffn_setup()
    _d = {'L0_attn_x': _L0_attn_in['x'], 'L0_attn_W_Q': _L0_attn_in['W_Q'], 'L0_attn_W_K': _L0_attn_in['W_K'], 'L0_attn_W_V': _L0_attn_in['W_V'], 'L0_attn_W_O': _L0_attn_in['W_O'], 'L0_ffn_w1': _L0_ffn_in['w1'], 'L0_ffn_w3': _L0_ffn_in['w3'], 'L0_ffn_w2': _L0_ffn_in['w2']}
    _x0 = _d['L0_attn_x']
    _d['L0_attn_x'] = jax.random.normal(jax.random.fold_in(jax.random.key(seed), 1), (2, 1024, 512), dtype=_x0.dtype)
    del _x0
    return _d

def reference(L0_attn_x, L0_attn_W_Q, L0_attn_W_K, L0_attn_W_V, L0_attn_W_O, L0_ffn_w1, L0_ffn_w3, L0_ffn_w2):

    def _L0_attn_ref(x, W_Q, W_K, W_V, W_O):
        import jax, jax.numpy as jnp
        import numpy as np
        import math
        D_MODEL = 512
        N_HEADS = 16
        D_HEAD = 128
        BATCH = 2
        SEQ = 512
        d_head = W_Q.shape[1]
        seq_len = x.shape[1]
        scale = 1.0 / math.sqrt(d_head)
        q = jnp.einsum('bsd,hed->bhse', x, W_Q)
        k = jnp.einsum('bsd,hed->bhse', x, W_K)
        v = jnp.einsum('bsd,hed->bhse', x, W_V)
        scores = jnp.einsum('bhse,bhme->bhsm', q, k) * scale
        causal = jnp.triu(jnp.ones((seq_len, seq_len), dtype=bool), k=1)
        scores = jnp.where(causal, jnp.float32(-1000000000.0), scores)
        pattern = jax.nn.softmax(scores, axis=-1)
        z = jnp.einsum('bhsm,bhme->bhse', pattern, v)
        out = jnp.einsum('bhse,hde->bsd', z, W_O)
        return out

    def _L0_ffn_ref(x, w1, w3, w2):
        import jax, jax.numpy as jnp
        import numpy as np
        D_MODEL = 512
        HIDDEN = int(2 * D_MODEL * 4 / 3)

        def ternary_quant(w):
            s = jnp.mean(jnp.abs(w))
            q = jnp.clip(jnp.round(w / s), -1.0, 1.0) * s
            return w + jax.lax.stop_gradient(q - w)
        w1q = ternary_quant(w1)
        w3q = ternary_quant(w3)
        w2q = ternary_quant(w2)
        h1 = jnp.einsum('bsd,hd->bsh', x, w1q)
        h3 = jnp.einsum('bsd,hd->bsh', x, w3q)
        g = jax.nn.silu(h1) * h3
        return jnp.einsum('bsh,dh->bsd', g, w2q)
    x = L0_attn_x
    x = x + _layernorm(_L0_attn_ref(_layernorm(x, axis=-1), L0_attn_W_Q, L0_attn_W_K, L0_attn_W_V, L0_attn_W_O), axis=-1)
    x = x + _layernorm(_L0_ffn_ref(_layernorm(x, axis=-1), L0_ffn_w1, L0_ffn_w3, L0_ffn_w2), axis=-1)
    return x

_drawn_inputs = setup_inputs


def setup_inputs(seed=0):
    import zlib

    import numpy as np

    out = dict(_drawn_inputs(seed))
    spreads = {}
    factors = {}
    for name, (base, spread) in spreads.items():
        noise = np.random.default_rng([zlib.crc32(name.encode()), seed]).standard_normal(out[name].shape)
        drawn = base * np.exp(spread * noise) if base else spread * noise
        out[name] = jnp.asarray(drawn.astype(out[name].dtype))
    for name, factor in factors.items():
        out[name] = (out[name] * factor).astype(out[name].dtype)
    return out
```

```python
from contextlib import ExitStack

import concourse.bass as bass
from concourse import mybir

ALU = mybir.AluOpType
ACT = mybir.ActivationFunctionType
AX = mybir.AxisListType
F32 = mybir.dt.float32
F32R = mybir.dt.float32r
BF16 = mybir.dt.bfloat16

P = 128
BATCH, SEQ, D = 2, 1024, 512
HEADS, E = 16, 128
HIDDEN = int(2 * D * 4 / 3)
C = D // P
QT = SEQ // P
TOK = BATCH * SEQ
XT = TOK // P
NH = BATCH * HEADS
BODY = 4
TURNS = (NH - BODY) // BODY
HALF = 512
MC = -(-HIDDEN // P)
G = TOK // HALF
GT = HALF // P
QUADS = NH // BODY
SCALE = float(E) ** -0.5
MASKED = -1.0e9 / SCALE
EPS = 1e-5

WIDTH = [256, 256, 384, 512]
FILL = [0, 1, 2, 3, 4, 6, 8, 10]
FILLS = 12

FULL = [["S", "K0", "T7", "O"], ["S", "K1", "PV1", "T0", "O"], ["S", "T1", "V0", "O"], ["S", "T2", "V1", "VA", "O", "T3"],
        ["S", "VB", "O"], ["S", "PV0", "T4", "O"], ["S", "Q0", "T5", "O"], ["S", "Q1", "T6", "O"]]
FIRST = [[op for op in s if op not in ("T7", "PV1", "O")] for s in FULL]
LAST = [[op for op in s if op[0] not in "KVQ"] for s in FULL]
TAIL = [["T7", "O"], ["O"], ["PV1", "O"]] + [["O"]] * 5
PROJ = {"K0": 1, "K1": 2, "V0": 3, "V1": 4, "Q0": 5, "Q1": 6}
PROJ_HI = {"K0": 1, "K1": 2, "Q0": 3, "Q1": 4}

ACC_BANK = {"K0": 0, "O0": 1, "K1": 0, "PV1": 1, "O1": 0, "V0": 1, "O2": 0, "V1": 1, "O3": 0, "O4": 1,
            "PV0": 0, "O5": 1, "Q0": 0, "O6": 1, "Q1": 0, "O7": 1}
ACC_BEFORE = {"K0": "Q1-", "O0": "O7-", "K1": "K0", "PV1": "O0", "O1": "K1", "V0": "PV1", "O2": "O1", "V1": "V0",
              "O3": "O2", "O4": "V1", "PV0": "O3", "O5": "O4", "Q0": "PV0", "O6": "O5", "Q1": "Q0", "O7": "O6"}
ACC_BEFORE_FIRST = {"K0": "Q1-", "K1": "K0", "V0": "Q1-", "V1": "V0", "PV0": "K1", "Q0": "PV0", "Q1": "Q0"}
ACC_BEFORE_LAST = {**ACC_BEFORE, "O1": "Q1-", "O4": "PV1"}
ACC_BEFORE_TAIL = {"O0": "O7-", "O1": "PV0-", "PV1": "O0", "O2": "O1", "O3": "O2", "O4": "PV1", "O5": "O4",
                   "O6": "O5", "O7": "O6"}
TP_BEFORE = {("T7", 0): ("T6-", 0), ("T7", 1): ("T6-", 1), ("T0", 0): ("T7", 0), ("T1", 1): ("T7", 1),
             ("VA", 1): ("T1", 1), ("T2", 0): ("T0", 0), ("T3", 0): ("T2", 0), ("VB", 1): ("VA", 1),
             ("T4", 0): ("T3", 0), ("T4", 1): ("VB", 1), ("T5", 0): ("T4", 0), ("T5", 1): ("T4", 1),
             ("T6", 0): ("T5", 0), ("T6", 1): ("T5", 1)}
ONE_BANK = {"T0": 0, "T1": 1, "T2": 0, "T3": 0, "VA": 1, "VB": 1}


class Head:

    def __init__(self, n, turn=None, steps=FULL, before=ACC_BEFORE):
        self.n, self.turn, self.steps, self.before = n, turn, steps, before

    def at(self, per_head, offset):
        fixed = per_head * self.n + offset
        return fixed if self.turn is None else self.turn * (BODY * per_head) + fixed

    def slot(self, n):
        return (self.n + n) % 2


def heads_of(eng):
    yield Head(0, steps=FIRST, before=ACC_BEFORE_FIRST)
    with eng.Fori(0, TURNS) as turn:
        for k in range(BODY):
            yield Head(1 + k, turn)
    for n in range(1 + BODY * TURNS, NH - 1):
        yield Head(n)
    yield Head(NH - 1, steps=LAST, before=ACC_BEFORE_LAST)
    yield Head(NH, steps=TAIL, before=ACC_BEFORE_TAIL)


def block_kernel(nc, x, wq, wk, wv, wo, w1, w3, w2, out):
    ctx = ExitStack()
    with ctx:
        def sem(name):
            return ctx.enter_context(nc.semaphore(name))

        R_COLS = 2 * C * TOK + 5 * 2 * C * E + 2 * 2 * SEQ + 2 * SEQ + 2 * 2 * SEQ + 2 * SEQ + 2 * QT * HALF
        F_COLS = 4 * 512 + 2 * SEQ + QT * D + SEQ
        arena_r = ctx.enter_context(nc.sbuf_tensor("arena_r", [P, R_COLS], F32R))
        arena_f = ctx.enter_context(nc.sbuf_tensor("arena_f", [P, F_COLS], F32))
        taken = {"r": 0, "f": 0}

        def take(which, *shape):
            n = 1
            for s in shape:
                n *= s
            a = (arena_r if which == "r" else arena_f)[:, taken[which]:taken[which] + n]
            taken[which] += n
            assert taken[which] <= (R_COLS if which == "r" else F_COLS)
            names = "abcd"[:len(shape)]
            sizes = {names[i]: shape[i] for i in range(1, len(shape))}
            return a.rearrange(f"p ({' '.join(names)}) -> p {' '.join(names)}", **sizes)

        def f32(ap):
            return ap.bitcast(F32)

        xnt = take("r", 2, C, TOK)
        w_k, w_v, w_q = (take("r", 2, C, E) for _ in range(3))
        w_o = take("r", 2, 2, C * E)
        kt = take("r", 2, 2, SEQ)
        qt = take("r", 2, SEQ)
        v = take("r", 2, 2, QT * E)
        zt = take("r", 2, SEQ)
        pt = take("r", 2, QT, HALF)
        raw_k, raw_v, raw_q, raw_o = (take("f", D) for _ in range(4))
        probs = take("f", 2, SEQ)
        acc = take("f", QT, D)
        vt = take("f", SEQ)
        xin = probs.rearrange("p a (b d) -> p (a b) d", d=D)

        taken["r"] = taken["f"] = 0
        w1t, w3t = take("r", MC, C, P), take("r", MC, C, P)
        w2t = take("r", MC, D)
        x1nt = take("r", 2, C, HALF)
        gt = take("r", 2, MC, HALF)
        x1_next, x1_now = take("f", GT, D), take("f", GT, D)
        stage = take("f", C + 1, D)
        gate = take("f", D)
        ghid = take("f", D)
        wraw = stage
        junk = take("f", D)
        x1n = take("f", 2, D)
        fin = junk

        small = ctx.enter_context(nc.sbuf_tensor("small", [P, 160], F32))
        negmax, rowsum, rinv = small[:, 0:8], small[:, 8:16], small[:, 16:24]
        stats = small[:, 24:36].rearrange("p (a b) -> p a b", b=6)
        mv = small[:, 36:40].rearrange("p (a b) -> p a b", b=2)
        varp = small[:, 40:42]
        rstd = small[:, 42:44]
        power = small[:, 44:45]
        totals = small[:, 48:51]
        scales = small[:, 51:54]
        above = small[:, 54:57]
        below = small[:, 57:60]
        stats3 = small[:, 60:66]
        mv3 = small[:, 66:68]
        rstd3 = small[:, 68:69]
        shift3 = small[:, 69:70]
        scaled3 = small[:, 70:71]
        squared = small[:, 71:72]
        abssum = small[:, 80:80 + 3 * MC]
        identity = ctx.enter_context(nc.sbuf_tensor("identity", [P, P], F32))
        ones = ctx.enter_context(nc.sbuf_tensor("ones", [P, P], F32))
        identity_b = ctx.enter_context(nc.sbuf_tensor("identity_b", [P, P], BF16))
        mask = ctx.enter_context(nc.sbuf_tensor("mask", [P, P], BF16))

        score = [ctx.enter_context(nc.psum_tensor(f"score{i}", [P, SEQ], F32)) for i in range(2)]
        tp = [ctx.enter_context(nc.psum_tensor(f"tp{i}", [P, HALF], F32)) for i in range(2)]
        accum = [ctx.enter_context(nc.psum_tensor(f"accum{i}", [P, HALF], F32)) for i in range(2)]

        partial = nc.dram_tensor("partial", [QUADS, P, QT, D], F32, kind="Internal").ap()

        s_const = sem("s_const")
        s_mask = sem("s_mask")
        s_xin = [sem(f"s_xin{i}") for i in range(4)]
        s_bn, s_var = sem("s_bn"), sem("s_var")
        s_eps, s_rstd = sem("s_eps"), sem("s_rstd")
        s_xn = sem("s_xn")
        s_xt, s_xhi, s_xlo = sem("s_xt"), sem("s_xhi"), sem("s_xlo")
        s_raw = {w: sem(f"s_raw_{w}") for w in "kvqo"}
        s_split_hi = {w: sem(f"s_split_hi_{w}") for w in "kvqo"}
        s_split = {w: sem(f"s_split_{w}") for w in "kvqo"}
        s_proj, s_projhi, s_projlo = sem("s_proj"), sem("s_projhi"), sem("s_projlo")
        s_vt, s_vhi, s_vlo = sem("s_vt"), sem("s_vhi"), sem("s_vlo")
        s_score, s_negmax, s_exp = sem("s_score"), sem("s_negmax"), sem("s_exp")
        s_rinv, s_norm = sem("s_rinv"), sem("s_norm")
        s_t, s_thi, s_tlo = sem("s_t"), sem("s_thi"), sem("s_tlo")
        s_pv, s_zhi, s_zlo = sem("s_pv"), sem("s_zhi"), sem("s_zlo")
        s_o = sem("s_o")
        s_sum = sem("s_sum")
        s_part = sem("s_part")
        s_accfree = sem("s_accfree")
        s_passed = [sem("s_passed_pool"), sem("s_passed_dve")]
        s_ptzero = sem("s_ptzero")
        s_w = [sem(f"s_w{i}") for i in range(4)]
        s_abs = sem("s_abs")
        s_tot, s_mean, s_thr = sem("s_tot"), sem("s_mean"), sem("s_thr")
        s_less, s_tern = sem("s_less"), sem("s_tern")
        s_stage = sem("s_stage")
        s_psum = sem("s_psum")
        s_fbn, s_fvar, s_feps, s_frstd = sem("s_fbn"), sem("s_fvar"), sem("s_feps"), sem("s_frstd")
        s_y, s_x1 = sem("s_y"), sem("s_x1")
        s_x1n, s_x1t = sem("s_x1n"), sem("s_x1t")
        s_x1hi, s_x1lo = sem("s_x1hi"), sem("s_x1lo")
        s_now = sem("s_now")
        s_h, s_silu, s_gated, s_ghi, s_glo = (sem(f"s_{n}") for n in ("h", "silu", "gated", "ghi", "glo"))
        s_f = sem("s_f")
        s_obn, s_ovar, s_oeps, s_orstd = sem("s_obn"), sem("s_ovar"), sem("s_oeps"), sem("s_orstd")
        s_oscale = sem("s_oscale")
        s_oshift, s_onorm, s_fin, s_out = sem("s_oshift"), sem("s_onorm"), sem("s_fin"), sem("s_out")

        block = ctx.enter_context(nc.Block())

        def fill(h, i, second=False):
            return h.at(FILLS, FILL[i] + 1 + second)

        def key_slot(group, j):
            return QT - 1 if j == 4 * group + 3 else j

        def alone(eng, which):
            eng.sem_inc(s_passed[which], 1)

        def tile_of(op):
            return int(op[1:])

        def fills_of(op):
            if op in ONE_BANK:
                return [(ONE_BANK[op], 0, 4 if op[0] == "V" else tile_of(op) + 1)]
            return [(0, 0, 4), (1, 4, tile_of(op) - 3)]

        def pt_block(hilo, i, j0, n):
            q = slice(i % 4 * P, (i % 4 + 1) * P)
            js = list(range(j0, j0 + n))
            last = 4 * (i // 4) + 3
            runs = []
            if last in js and key_slot(i // 4, last) != last:
                js.remove(last)
                runs = [(last - j0, 1, pt[:, hilo, QT - 1:QT, q])]
            return [(js[0] - j0, len(js), pt[:, hilo, js[0]:js[0] + len(js), q])] + runs

        @block.sync
        def _(sp):
            def load(w, src, head):
                dst = {"k": raw_k, "v": raw_v, "q": raw_q, "o": raw_o}[w]
                sp.dma_start(dst, src[head]).then_inc(s_raw[w], 16)

            def load_x(n):
                if n >= 4:
                    sp.wait_ge(s_xt, n - 3)
                sp.dma_start(xin[:, n % 4, :], x[n * P:(n + 1) * P, :]).then_inc(s_xin[n % 4], 16)

            for n in range(4):
                load_x(n)
            load("k", wk, 0)
            load("v", wv, 0)
            load("q", wq, 0)
            load("o", wo, 0)
            for n in range(4, 8):
                load_x(n)
            sp.wait_ge(s_split["k"], 1)
            load("k", wk, 1)
            sp.wait_ge(s_split["v"], 1)
            load("v", wv, 1)
            sp.wait_ge(s_split["q"], 1)
            load("q", wq, 1)
            for n in range(8, XT):
                load_x(n)
            sp.wait_ge(s_split["k"], 2)
            load("k", wk, 2)
            sp.wait_ge(s_split["v"], 2)
            load("v", wv, 2)
            sp.sem_inc(s_accfree, 1)
            for h in heads_of(sp):
                last = h.turn is None
                if not (last and h.n + 2 > NH - 1):
                    sp.wait_ge(s_split["q"], h.at(1, 2))
                    load("q", wq, h.at(1, 2) % HEADS)
                if not (last and h.n + 3 > NH - 1):
                    sp.wait_ge(s_split["k"], h.at(1, 3))
                    load("k", wk, h.at(1, 3) % HEADS)
                    sp.wait_ge(s_split["v"], h.at(1, 3))
                    load("v", wv, h.at(1, 3) % HEADS)
                if h.n % BODY == 0 and not (last and h.n == 0):
                    quad = h.turn if h.turn is not None else QUADS - 1
                    sp.wait_ge(s_sum, h.at(QT, 4))
                    sp.dma_start(partial[quad, :, 0:4, :], acc[:, 0:4, :]).then_inc(s_part, 16)
                if not (last and h.n + 1 > NH - 1):
                    sp.wait_ge(s_split["o"], h.at(1, 1))
                    load("o", wo, h.at(1, 1) % HEADS)
                if h.n % BODY == 0 and not (last and h.n == 0):
                    sp.wait_ge(s_sum, h.at(QT, 8))
                    sp.dma_start(partial[quad, :, 4:8, :], acc[:, 4:8, :]).then_inc(s_part, 16)
                    sp.wait_ge(s_part, 32 * (quad + 1) if last else h.turn * 32 + 32)
                    sp.sem_inc(s_accfree, 1)

            pieces = [(w1, m) for m in range(MC)] + [(w3, m) for m in range(MC)] + [(w2, m) for m in range(MC)]
            for n, (w, m) in enumerate(pieces):
                if n >= 4:
                    sp.wait_ge(s_abs, n - 3)
                sp.dma_start(wraw[:, n % 4, :], w[:, m, :]).then_inc(s_w[n % 4], 16)
            pieces = [p for m in range(MC) for p in ((w1, m), (w3, m))] + [(w2, m) for m in range(MC)]
            for n, (w, m) in enumerate(pieces, 3 * MC):
                if n - 4 < 3 * MC:
                    sp.wait_ge(s_abs, n - 3)
                else:
                    sp.wait_ge(s_tern, n - 3 - 3 * MC)
                sp.dma_start(wraw[:, n % 4, :], w[:, m, :]).then_inc(s_w[n % 4], 16)
            sp.wait_ge(s_tern, 3 * MC)

            def load_tile(j, quad, row, rows, count, first):
                if not first:
                    sp.wait_ge(s_x1, count)
                sp.dma_start(stage[:, 0:C, :], partial[bass.ds(quad, 4), :, row, :].rearrange("q p d -> p q d")
                             ).then_inc(s_stage, 16)
                sp.dma_start(stage[:, C, :], x[bass.ds(rows, P), :]).then_inc(s_stage, 16)

            for j in range(GT):
                load_tile(j, 0, j, j * P, j, j == 0)
            def next_group(g):
                b = (g + 1) // 2
                half = (g + 1) % 2
                for j in range(GT):
                    sp.wait_ge(s_x1, g * GT + GT + j)
                    sp.dma_start(stage[:, 0:C, :], partial[bass.ds(b * 4, 4), :, bass.ds(half * 4 + j, 1), :]
                                 .rearrange("q p a d -> p q (a d)")).then_inc(s_stage, 16)
                    sp.dma_start(stage[:, C, :], x[bass.ds(g * HALF + (HALF + j * P), P), :]).then_inc(s_stage, 16)

            def store(g):
                for j in range(GT):
                    sp.wait_ge(s_fin, g * GT + (j + 1))
                    sp.dma_start(out[bass.ds(g * HALF + j * P, P), :], fin).then_inc(s_out, 16)

            with sp.Fori(0, G - 1) as g:
                next_group(g)
                store(g)
            store(G - 1)
            sp.wait_ge(s_out, 16 * G * GT)

        @block.gpsimd
        def _(pool):
            nc.gpsimd.memset(identity[:, :], 0.0).then_inc(s_mask, 1)
            nc.gpsimd.memset(mask[:, :], 0.0).then_inc(s_mask, 1)
            nc.gpsimd.memset(identity_b[:, :], 0.0).then_inc(s_mask, 1)
            nc.gpsimd.memset(power, -0.5).then_inc(s_mask, 1)
            nc.gpsimd.memset(ones[:, :], 1.0).then_inc(s_const, 1)
            pool.wait_ge(s_mask, 4)
            for m in (identity, identity_b):
                nc.gpsimd.affine_select(out=m[:, :], in_=m[:, :], compare_op=ALU.not_equal, fill=1.0, base=0,
                                        pattern=[[-1, P]], channel_multiplier=1).then_inc(s_const, 1)
            nc.gpsimd.affine_select(out=mask[:, :], in_=mask[:, :], compare_op=ALU.is_ge, fill=MASKED, base=0,
                                    pattern=[[-1, P]], channel_multiplier=1).then_inc(s_const, 1)

            def rsqrt(n):
                pool.wait_ge(s_var, n + 1)
                nc.gpsimd.tensor_scalar(varp[:, n % 2:n % 2 + 1], mv[:, n % 2, 1:2], EPS, None, ALU.add
                                        ).then_inc(s_eps, 1)
                pool.wait_ge(s_eps, n + 1)
                nc.gpsimd.tensor_tensor(rstd[:, n % 2:n % 2 + 1], varp[:, n % 2:n % 2 + 1], power, ALU.pow
                                        ).then_inc(s_rstd, 1)

            def split(w, raw_count, count):
                raw = {"k": raw_k, "v": raw_v, "q": raw_q, "o": raw_o}[w[0]]
                dst = {"k": w_k, "v": w_v, "q": w_q}.get(w[0])
                hi, lo = ((w_o[:, w[1], p, :] for p in range(2)) if dst is None
                          else (dst[:, p, :, :].rearrange("p c e -> p (c e)") for p in range(2)))
                pool.wait_ge(s_raw[w[0]], raw_count)
                alone(pool, 0)
                nc.gpsimd.tensor_copy(hi, raw).then_inc(s_split_hi[w[0]], 1)
                pool.wait_ge(s_split_hi[w[0]], count)
                nc.gpsimd.tensor_tensor(lo, raw, f32(hi), ALU.subtract).then_inc(s_split[w[0]], 1)

            for n in range(8):
                rsqrt(n)
                if n == 2:
                    split("k", 16, 1)
                if n == 4:
                    split("v", 16, 1)
                if n == 6:
                    split("q", 16, 1)
            for n in range(8, XT):
                rsqrt(n)
            pool.wait_ge(s_proj, 2)
            split("k", 32, 2)
            pool.wait_ge(s_proj, 4)
            split("v", 32, 2)

            for h in heads_of(pool):
                if h.n == NH:
                    break
                fixed = h.turn is None
                for i in range(QT):
                    pool.wait_ge(s_rinv, h.at(QT, i + 1))
                    alone(pool, 0)
                    pr = probs[:, i % 2, 0:(i + 1) * P]
                    nc.gpsimd.tensor_scalar(pr, pr, rinv[:, i:i + 1], 1.0, ALU.mult, ALU.mult).then_inc(s_norm, 1)
                    if i == 0 and not (fixed and h.n + 1 > NH - 1):
                        pool.wait_ge(s_proj, h.at(6, 6))
                        split("q", h.at(16, 32), h.at(1, 2))
                    if i == 2 and not (fixed and h.n + 2 > NH - 1):
                        pool.wait_ge(s_proj, h.at(6, 8))
                        split("k", h.at(16, 48), h.at(1, 3))
                    if i == 4 and not (fixed and h.n + 2 > NH - 1):
                        pool.wait_ge(s_proj, h.at(6, 10))
                        split("v", h.at(16, 48), h.at(1, 3))
                    if i == 6:
                        split(("o", h.slot(0)), h.at(16, 16), h.at(1, 1))

            def first_half(j, count):
                pool.wait_ge(s_stage, count(32, 32))
                for q in range(1, C):
                    nc.gpsimd.tensor_tensor(stage[:, 0, :], stage[:, 0, :], stage[:, q, :], ALU.add
                                            ).then_inc(s_psum, 1)
                    if q < C - 1:
                        pool.wait_ge(s_psum, count(3, q))

            def ffn_rsqrt(count):
                pool.wait_ge(s_fvar, count)
                alone(pool, 0)
                nc.gpsimd.tensor_scalar(varp[:, 0:1], mv[:, 0, 1:2], EPS, None, ALU.add).then_inc(s_feps, 1)
                pool.wait_ge(s_feps, count)
                nc.gpsimd.tensor_tensor(rstd[:, 0:1], varp[:, 0:1], power, ALU.pow).then_inc(s_frstd, 1)

            def prepare(g, j):
                def count(per, off):
                    return per * j + off if g is None else g * (per * GT) + (per * (GT + j) + off)
                first_half(j, count)
                ffn_rsqrt(count(2, 1))
                ffn_rsqrt(count(2, 2))

            for j in range(GT):
                prepare(None, j)

            def finish(g, j):
                at = lambda off: g * GT + (j + off)
                pool.wait_ge(s_ovar, at(1))
                alone(pool, 0)
                nc.gpsimd.tensor_scalar(scaled3, mv3[:, 1:2], squared, EPS, ALU.mult, ALU.add).then_inc(s_oeps, 1)
                pool.wait_ge(s_oeps, at(1))
                nc.gpsimd.tensor_tensor(rstd3, scaled3, power, ALU.pow).then_inc(s_orstd, 1)
                pool.wait_ge(s_onorm, at(1))
                nc.gpsimd.tensor_tensor(fin, fin, x1_now[:, j, :], ALU.add).then_inc(s_fin, 1)
                pool.wait_ge(s_fin, at(1))

            def keep(g):
                nc.gpsimd.tensor_copy(x1_now[:, :, :], x1_next[:, :, :]).then_inc(s_now, 1)

            with pool.Fori(0, G - 1) as g:
                pool.wait_ge(s_x1n, g * GT + GT)
                alone(pool, 0)
                keep(g)
                for j in range(GT):
                    prepare(g, j)
                for j in range(GT):
                    finish(g, j)
            pool.wait_ge(s_x1n, G * GT)
            keep(G - 1)
            for j in range(GT):
                finish(G - 1, j)

        @block.scalar
        def _(act):
            def x_hi(n):
                act.wait_ge(s_xt, n + 1)
                nc.scalar.activation(xnt[:, 0, :, n * P:(n + 1) * P], tp[n % 2][:, :].rearrange("p (c q) -> p c q", c=C),
                                     ACT.Copy).then_inc(s_xhi, 1)

            def proj_hi(op, slot, count, hi_count, bank):
                half = slice(int(op[1]) * HALF, (int(op[1]) + 1) * HALF)
                act.wait_ge(s_proj, count)
                dst = kt[:, slot, 0, half] if op[0] == "K" else qt[:, 0, half]
                nc.scalar.activation(dst, accum[bank][:, :], ACT.Copy, scale=1.0 if op[0] == "K" else SCALE
                                     ).then_inc(s_projhi, 1)

            def v_hi(op, slot, count, bank):
                half = slice(HALF * (op == "VB"), HALF * (op == "VB") + HALF)
                act.wait_ge(s_vt, count)
                nc.scalar.activation(v[:, slot, 0, half], tp[bank][:, :], ACT.Copy).then_inc(s_vhi, 1)

            for n in range(8):
                x_hi(n)
            for n, op in enumerate(("K0", "K1")):
                proj_hi(op, 0, PROJ[op], PROJ_HI[op], n % 2)
            for n in range(8, 12):
                x_hi(n)
            v_hi("VA", 0, 1, 0)
            v_hi("VB", 0, 2, 1)
            for n, op in enumerate(("Q0", "Q1")):
                proj_hi(op, 0, PROJ[op], PROJ_HI[op], n % 2)
            for n in range(12, XT):
                x_hi(n)

            for h in heads_of(act):
                for i, step in enumerate(h.steps):
                    if "S" in step:
                        act.wait_ge(s_negmax, h.at(QT, i + 1))
                        if i >= 2 or h.n > 0:
                            before = fill(h, i - 2, i - 2 >= 4) if i >= 2 else h.at(FILLS, (-2, 0)[i])
                            act.wait_ge(s_t, before)
                        nc.scalar.activation(probs[:, i % 2, 0:(i + 1) * P], score[i % 2][:, 0:(i + 1) * P], ACT.Exp,
                                             bias=negmax[:, i:i + 1], scale=1.0,
                                             accum_out=rowsum[:, i:i + 1]).then_inc(s_exp, 1)
                    for op in step:
                        if op in PROJ_HI:
                            proj_hi(op, h.slot(1), h.at(6, 6 + PROJ[op]), None, ACC_BANK[op])
                        elif op in ("VA", "VB"):
                            v_hi(op, h.slot(1), h.at(2, 3 + (op == "VB")), 1)
                        elif op in ("PV0", "PV1"):
                            half = slice(int(op[2]) * HALF, (int(op[2]) + 1) * HALF)
                            act.wait_ge(s_pv, h.at(2, 1 if op == "PV0" else 0))
                            nc.scalar.activation(zt[:, 0, half], accum[ACC_BANK[op]][:, :], ACT.Copy).then_inc(s_zhi, 1)
                        elif op[0] == "T":
                            q = tile_of(op)
                            if q == 0 and h.n > 0:
                                act.wait_ge(s_pv, h.at(2, 0))
                            if q == 4:
                                act.wait_ge(s_pv, h.at(2, 1))
                            for f, (bank, j0, n) in enumerate(fills_of(op)):
                                act.wait_ge(s_t, h.at(FILLS, FILL[q] + 1 + f - (FILLS if q == 7 else 0)))
                                src = tp[bank][:, 0:n * P].rearrange("p (j q) -> p j q", q=P)
                                for k, (at, m, dst) in enumerate(pt_block(0, q, j0, n)):
                                    ins = nc.scalar.activation(dst, src[:, at:at + m, :], ACT.Copy)
                                ins.then_inc(s_thi, 1)

            act.wait_ge(s_accfree, QUADS + 1)
            for n in range(3 * MC):
                act.wait_ge(s_w[n % 4], 16 * (n // 4 + 1))
                if n:
                    act.wait_ge(s_abs, n)
                nc.scalar.activation(junk, wraw[:, n % 4, :], ACT.Abs, accum_out=abssum[:, n:n + 1]).then_inc(s_abs, 1)

            def x1_hi(j, count):
                act.wait_ge(s_x1t, count)
                nc.scalar.activation(x1nt[:, 0, :, j * P:(j + 1) * P],
                                     score[(j // 2 + 1) % 2][:, j % 2 * HALF:(j % 2 + 1) * HALF]
                                     .rearrange("p (c q) -> p c q", c=C), ACT.Copy).then_inc(s_x1hi, 1)

            for j in range(GT):
                x1_hi(j, j + 1)

            def group(g, more):
                at = lambda per, off: g * per + off
                for m in range(MC):
                    act.wait_ge(s_h, at(MC, m + 1))
                    nc.scalar.activation(gate, score[m % 2][:, 0:HALF], ACT.Silu, scale=scales[:, 0:1]).then_inc(s_silu, 1)
                    act.wait_ge(s_gated, at(MC, m + 1))
                    nc.scalar.activation(gt[:, 0, m, :], ghid, ACT.Copy).then_inc(s_ghi, 1)
                if more:
                    for j in range(GT):
                        x1_hi(j, at(GT, GT + j + 1))
                for j in range(GT):
                    act.wait_ge(s_oshift, at(GT, j + 1))
                    nc.scalar.activation(fin, ff_bank(j), ACT.Identity, bias=shift3, scale=rstd3).then_inc(s_onorm, 1)
                    act.wait_ge(s_out, at(GT * 16, 16 * (j + 1)))

            def ff_bank(j):
                return (tp + accum)[j][:, :]

            with act.Fori(0, G - 1) as g:
                group(g, True)
            group(G - 1, False)

        @block.vector
        def _(dve):
            nc.vector.memset(f32(pt[:, :, QT - 1, 2 * P:3 * P]), 0.0).then_inc(s_ptzero, 1)
            dve.sem_inc(s_sum, QT)

            def x_stats(n):
                dve.wait_ge(s_xin[n % 4], 16 * (n // 4 + 1))
                nc.vector.bn_stats(stats[:, n % 2, :], xin[:, n % 4, :]).then_inc(s_bn, 1)
                dve.wait_ge(s_bn, n + 1)
                nc.vector.bn_aggr(mv[:, n % 2, :], stats[:, n % 2, :]).then_inc(s_var, 1)

            def x_norm(n):
                dve.wait_ge(s_rstd, n + 1)
                nc.vector.tensor_scalar(xin[:, n % 4, :], xin[:, n % 4, :], mv[:, n % 2, 0:1],
                                        rstd[:, n % 2:n % 2 + 1], ALU.subtract, ALU.mult).then_inc(s_xn, 1)

            def x_lo(n):
                dve.wait_ge(s_xhi, n + 1)
                cols = slice(n * P, (n + 1) * P)
                nc.vector.tensor_tensor(xnt[:, 1, :, cols], tp[n % 2][:, :].rearrange("p (c q) -> p c q", c=C),
                                        f32(xnt[:, 0, :, cols]), ALU.subtract).then_inc(s_xlo, 1)

            def proj_lo(op, slot, count, hi_count, bank):
                half = slice(int(op[1]) * HALF, (int(op[1]) + 1) * HALF)
                if op[0] == "V":
                    dve.wait_ge(s_proj, count)
                    nc.vector.tensor_copy(vt[:, half], accum[bank][:, :]).then_inc(s_projlo, 1)
                    return
                dve.wait_ge(s_projhi, hi_count)
                if op[0] == "K":
                    nc.vector.tensor_tensor(kt[:, slot, 1, half], accum[bank][:, :], f32(kt[:, slot, 0, half]),
                                            ALU.subtract).then_inc(s_projlo, 1)
                else:
                    nc.vector.scalar_tensor_tensor(qt[:, 1, half], accum[bank][:, :], SCALE, f32(qt[:, 0, half]),
                                                   ALU.mult, ALU.subtract).then_inc(s_projlo, 1)

            def v_lo(op, slot, count, bank):
                half = slice(HALF * (op == "VB"), HALF * (op == "VB") + HALF)
                dve.wait_ge(s_vhi, count)
                nc.vector.tensor_tensor(v[:, slot, 1, half], tp[bank][:, :], f32(v[:, slot, 0, half]),
                                        ALU.subtract).then_inc(s_vlo, 1)

            x_stats(0)
            x_stats(1)
            for n in range(8):
                x_norm(n)
                if n < 6:
                    x_stats(n + 2)
                if n:
                    x_lo(n - 1)
            x_lo(7)
            x_stats(8)
            x_stats(9)
            for n, op in enumerate(("K0", "K1", "V0", "V1")):
                proj_lo(op, 0, PROJ[op], PROJ_HI.get(op), n % 2)
                x_norm(8 + n)
                x_stats(10 + n)
            for n in range(8, 12):
                x_lo(n)
            v_lo("VA", 0, 1, 0)
            v_lo("VB", 0, 2, 1)
            for n, op in enumerate(("Q0", "Q1")):
                proj_lo(op, 0, PROJ[op], PROJ_HI[op], n % 2)
                x_norm(12 + n)
                x_stats(14 + n)
            x_norm(14)
            x_norm(15)
            for n in range(12, XT):
                x_lo(n)

            def add_out(h, i):
                dve.wait_ge(s_o, h.at(QT, i + 1 - QT))
                if (h.n - 1) % BODY == 0:
                    if i == 0:
                        dve.wait_ge(s_accfree, h.turn + 1 if h.turn is not None else QUADS)
                    nc.vector.tensor_copy(acc[:, i, :], accum[ACC_BANK[f"O{i}"]][:, :]).then_inc(s_sum, 1)
                else:
                    nc.vector.tensor_tensor(acc[:, i, :], accum[ACC_BANK[f"O{i}"]][:, :], acc[:, i, :], ALU.add
                                            ).then_inc(s_sum, 1)

            for h in heads_of(dve):
                for i, step in enumerate(h.steps):
                    if "S" in step:
                        dve.wait_ge(s_score, h.at(QT, i + 1))
                        nc.vector.tensor_reduce(negmax[:, i:i + 1], score[i % 2][:, 0:(i + 1) * P], AX.X, ALU.max,
                                                negate=True).then_inc(s_negmax, 1)
                    if i > 0 and "O" in h.steps[i - 1]:
                        add_out(h, i - 1)
                    if "S" in step:
                        dve.wait_ge(s_exp, h.at(QT, i + 1))
                        nc.vector.reciprocal(rinv[:, i:i + 1], rowsum[:, i:i + 1]).then_inc(s_rinv, 1)
                    for op in step:
                        if op in PROJ:
                            proj_lo(op, h.slot(1), h.at(6, 6 + PROJ[op]),
                                    h.at(4, 4 + PROJ_HI[op]) if op in PROJ_HI else None, ACC_BANK[op])
                        elif op in ("VA", "VB"):
                            v_lo(op, h.slot(1), h.at(2, 3 + (op == "VB")), 1)
                        elif op in ("PV0", "PV1"):
                            half = slice(int(op[2]) * HALF, (int(op[2]) + 1) * HALF)
                            dve.wait_ge(s_zhi, h.at(2, 1 if op == "PV0" else 0))
                            nc.vector.tensor_tensor(zt[:, 1, half], accum[ACC_BANK[op]][:, :], f32(zt[:, 0, half]),
                                                    ALU.subtract).then_inc(s_zlo, 1)
                        elif op[0] == "T":
                            q = tile_of(op)
                            for f, (bank, j0, n) in enumerate(fills_of(op)):
                                dve.wait_ge(s_thi, h.at(FILLS, FILL[q] + 1 + f - (FILLS if q == 7 else 0)))
                                src = tp[bank][:, 0:n * P].rearrange("p (j q) -> p j q", q=P)
                                for (at, m, hi), (_, _, lo) in zip(pt_block(0, q, j0, n), pt_block(1, q, j0, n)):
                                    ins = nc.vector.tensor_tensor(lo, src[:, at:at + m, :], f32(hi), ALU.subtract)
                                ins.then_inc(s_tlo, 1)
                if "O" in h.steps[QT - 1]:
                    add_out(h, QT - 1)

            dve.wait_ge(s_abs, 3 * MC)
            nc.vector.tensor_reduce(totals, abssum.rearrange("p (w m) -> p w m", w=3), AX.X, ALU.add
                                    ).then_inc(s_tot, 1)
            dve.wait_ge(s_mean, 1)
            for dst, k in ((scales, 1.0), (above, 0.5), (below, -0.5)):
                nc.vector.tensor_scalar(dst, accum[0][:, 0:3], k / (HIDDEN * D), None, ALU.mult).then_inc(s_thr, 1)
            dve.wait_ge(s_thr, 3)
            nc.vector.tensor_tensor(squared, scales[:, 2:3], scales[:, 2:3], ALU.mult).then_inc(s_thr, 1)
            order = [p for m in range(MC) for p in ((0, w1t, m), (1, w3t, m))] + [(2, w2t, m) for m in range(MC)]
            for n, (w, dst, m) in enumerate(order):
                slot = (3 * MC + n) % 4
                dve.wait_ge(s_w[slot], 16 * ((3 * MC + n) // 4 + 1))
                if n:
                    dve.wait_ge(s_tern, n)
                nc.vector.tensor_scalar(junk, wraw[:, slot, :], below[:, w:w + 1], None, ALU.is_lt).then_inc(s_less, 1)
                dve.wait_ge(s_less, n + 1)
                d = dst[:, m, :, :].rearrange("p c h -> p (c h)") if w < 2 else dst[:, m, :]
                nc.vector.scalar_tensor_tensor(d, wraw[:, slot, :], above[:, w:w + 1], junk, ALU.is_gt, ALU.subtract
                                               ).then_inc(s_tern, 1)

            def normalise(dst, src, count):
                nc.vector.bn_stats(stats[:, 0, :], src).then_inc(s_fbn, 1)
                dve.wait_ge(s_fbn, count)
                alone(dve, 1)
                nc.vector.bn_aggr(mv[:, 0, :], stats[:, 0, :]).then_inc(s_fvar, 1)
                dve.wait_ge(s_frstd, count)
                return nc.vector.tensor_scalar(dst, src, mv[:, 0, 0:1], rstd[:, 0:1], ALU.subtract, ALU.mult)

            def prepare_a(g, j):
                count = lambda per, off: per * j + off if g is None else g * (per * GT) + (per * (GT + j) + off)
                dve.wait_ge(s_psum, count(3, 3))
                normalise(stage[:, 0, :], stage[:, 0, :], count(2, 1)).then_inc(s_y, 1)
                dve.wait_ge(s_y, count(1, 1))
                if j == 0 and g is not None:
                    dve.wait_ge(s_now, g + 1)
                nc.vector.tensor_tensor(x1_next[:, j, :], stage[:, 0, :], stage[:, C, :], ALU.add).then_inc(s_x1, 1)
                dve.wait_ge(s_x1, count(1, 1))

            def prepare_b(g, j):
                count = lambda per, off: per * j + off if g is None else g * (per * GT) + (per * (GT + j) + off)
                if j >= 2:
                    dve.wait_ge(s_x1t, count(1, -1))
                normalise(x1n[:, j % 2, :], x1_next[:, j, :], count(2, 2)).then_inc(s_x1n, 1)

            def x1_lo(j, count):
                dve.wait_ge(s_x1hi, count)
                cols = slice(j * P, (j + 1) * P)
                nc.vector.tensor_tensor(x1nt[:, 1, :, cols],
                                        score[(j // 2 + 1) % 2][:, j % 2 * HALF:(j % 2 + 1) * HALF]
                                        .rearrange("p (c q) -> p c q", c=C),
                                        f32(x1nt[:, 0, :, cols]), ALU.subtract).then_inc(s_x1lo, 1)

            for j in range(GT):
                prepare_a(None, j)
                prepare_b(None, j)
            for j in range(GT):
                x1_lo(j, j + 1)

            def group(g, more):
                at = lambda per, off: g * per + off
                for m in range(MC):
                    dve.wait_ge(s_silu, at(MC, m + 1))
                    if m:
                        dve.wait_ge(s_glo, at(MC, m))
                    nc.vector.scalar_tensor_tensor(ghid, score[m % 2][:, HALF:2 * HALF], scales[:, 1:2], gate,
                                                   ALU.mult, ALU.mult).then_inc(s_gated, 1)
                    dve.wait_ge(s_ghi, at(MC, m + 1))
                    nc.vector.tensor_tensor(gt[:, 1, m, :], ghid, f32(gt[:, 0, m, :]), ALU.subtract).then_inc(s_glo, 1)
                    if more and m in (1, 5):
                        prepare_a(g, m // 4)
                    if more and m in (3, 7):
                        prepare_b(g, m // 4)
                if more:
                    x1_lo(0, at(GT, GT + 1))
                    x1_lo(1, at(GT, GT + 2))
                    for j in range(2, GT):
                        prepare_a(g, j)
                        prepare_b(g, j)
                    for j in range(2, GT):
                        x1_lo(j, at(GT, GT + j + 1))
                for j in range(GT):
                    if j == 0:
                        dve.wait_ge(s_f, at(1, 1))
                    if j:
                        dve.wait_ge(s_onorm, at(GT, j))
                    nc.vector.bn_stats(stats3, ff_bank(j)).then_inc(s_obn, 1)
                    dve.wait_ge(s_obn, at(GT, j + 1))
                    alone(dve, 1)
                    nc.vector.bn_aggr(mv3, stats3).then_inc(s_ovar, 1)
                    dve.wait_ge(s_orstd, at(GT, j + 1))
                    nc.vector.tensor_tensor(rstd3, rstd3, scales[:, 2:3], ALU.mult).then_inc(s_oscale, 1)
                    dve.wait_ge(s_oscale, at(GT, j + 1))
                    nc.vector.tensor_scalar(shift3, mv3[:, 0:1], rstd3, -1.0, ALU.mult, ALU.mult).then_inc(s_oshift, 1)

            def ff_bank(j):
                return (tp + accum)[j][:, :]

            with dve.Fori(0, G - 1) as g:
                group(g, True)
            group(G - 1, False)

        @block.tensor
        def _(pe):
            pe.wait_ge(s_const, 4)

            def x_transpose(n, free):
                pe.wait_ge(s_xn, n + 1)
                if free:
                    pe.wait_ge(*free)
                for c in range(C):
                    ins = nc.tensor.transpose(tp[n % 2][:, c * P:(c + 1) * P], xin[:, n % 4, c * P:(c + 1) * P],
                                              identity[:, :])
                ins.then_inc(s_xt, 1)

            def project(op, cols, bank):
                w = {"K": w_k, "V": w_v, "Q": w_q}[op[0]]
                for c in range(C):
                    for k, (a, b) in enumerate(((0, 0), (0, 1), (1, 0))):
                        ins = nc.tensor.matmul(accum[bank][:, :], w[:, a, c, :], xnt[:, b, c, cols],
                                               start=(c == 0 and k == 0), stop=(c == C - 1 and k == 2))
                ins.then_inc(s_proj, 1)

            def v_transpose(op, bank):
                base = 4 * (op == "VB")
                for j in range(4):
                    ins = nc.tensor.transpose(tp[bank][:, j * P:(j + 1) * P], vt[:, (base + j) * P:(base + j + 1) * P],
                                              identity[:, :])
                ins.then_inc(s_vt, 1)

            for n in range(8):
                x_transpose(n, (s_xlo, n - 1) if n >= 2 else None)
            pe.wait_ge(s_xlo, 8)
            for n, op in enumerate(("K0", "K1", "V0", "V1")):
                pe.wait_ge(s_split[op[0].lower()], 1)
                if n >= 2:
                    pe.wait_ge(s_projlo, n - 1)
                project(op, slice((n % 2) * HALF, (n % 2 + 1) * HALF), n % 2)
            for n in range(8, 12):
                x_transpose(n, (s_xlo, n - 1))
            for n, op in enumerate(("VA", "VB")):
                pe.wait_ge(s_projlo, 4)
                pe.wait_ge(s_xlo, 11 + n)
                v_transpose(op, n)
            for n, op in enumerate(("Q0", "Q1")):
                pe.wait_ge(s_split["q"], 1)
                pe.wait_ge(s_projlo, 3 + n)
                project(op, slice(n * HALF, (n + 1) * HALF), n)
            for n in range(12, XT):
                x_transpose(n, (s_vlo, n - 11) if n < 14 else (s_xlo, n - 1))

            def acc_free(h, op):
                was = h.before[op]
                back = was.endswith("-")
                was = was.rstrip("-")
                if was in PROJ:
                    pe.wait_ge(s_projlo, h.at(6, PROJ[was] + (0 if back else 6)))
                elif was == "PV0":
                    pe.wait_ge(s_zlo, h.at(2, 1 - 2 * back))
                elif was == "PV1":
                    pe.wait_ge(s_zlo, h.at(2, 0))
                else:
                    pe.wait_ge(s_sum, h.at(QT, tile_of(was) + 1 - QT * back))

            def tp_free(h, op, bank):
                if h.n == 0 and op in ("T0", "T1"):
                    pe.wait_ge(s_xlo, XT)
                    return
                was, _ = TP_BEFORE[op, bank]
                if was == "VB" and h.steps is LAST:
                    was = "T1"
                if was[0] == "V":
                    pe.wait_ge(s_vlo, h.at(2, 3 + (was == "VB")))
                    return
                q = int(was[1])
                previous = q == 7 or was.endswith("-")
                pe.wait_ge(s_tlo, h.at(FILLS, FILL[q] + 1 + (bank == 1 and q >= 4) - FILLS * previous))

            def scores(h, i):
                if i == 0:
                    pe.wait_ge(s_projlo, h.at(6, PROJ["Q0"]))
                if i == 4:
                    pe.wait_ge(s_projlo, h.at(6, PROJ["Q1"]))
                if i >= 2 or h.n > 0:
                    pe.wait_ge(s_exp, h.at(QT, i - 1))
                dst, slot = score[i % 2], h.slot(0)
                q = slice(i * P, (i + 1) * P)
                banks = [(0, WIDTH[i])] if i < 4 else [(0, HALF), (HALF, HALF + WIDTH[i - 4])]
                for b, (k0, k1) in enumerate(banks):
                    for n, (a, c) in enumerate(((0, 0), (0, 1), (1, 0))):
                        nc.tensor.matmul(dst[:, k0:k1], qt[:, a, q], kt[:, slot, c, k0:k1],
                                         start=(n == 0), stop=(n == 2 and b < i // 4))
                nc.tensor.matmul(dst[:, i * P:(i + 1) * P], identity_b[:, :], mask[:, :], start=False, stop=True
                                 ).then_inc(s_score, 1)

            def p_transpose(h, op):
                q = tile_of(op)
                pe.wait_ge(s_norm, h.at(QT, q + 1 - (QT if q == 7 else 0)))
                for bank, j0, n in fills_of(op):
                    tp_free(h, op, bank)
                    for j in range(n):
                        ins = nc.tensor.transpose(tp[bank][:, j * P:(j + 1) * P],
                                                  probs[:, q % 2, (j0 + j) * P:(j0 + j + 1) * P], identity[:, :])
                    ins.then_inc(s_t, 1)

            def values(h, op):
                group = int(op[2])
                slot = h.slot(-1 if group else 0)
                back = FILLS if group else 0
                pe.wait_ge(s_tlo, h.at(FILLS, (FILL[7] + 2 if group else FILL[3] + 1) - back))
                if not group:
                    pe.wait_ge(s_vlo, h.at(2, 2))
                dst = accum[ACC_BANK[op]]
                tiles = 4 * group + 4
                for j in range(tiles):
                    first = max(0, j - 4 * group)
                    q = slice(min(first, 2) * P, HALF)
                    for n, (a, b) in enumerate(((0, 0), (0, 1), (1, 0))):
                        ins = nc.tensor.matmul(dst[:, q], v[:, slot, a, j * P:(j + 1) * P],
                                               pt[:, b, key_slot(group, j), q],
                                               start=(j == 0 and n == 0), stop=(j == tiles - 1 and n == 2))
                ins.then_inc(s_pv, 1)

            def output(h, i):
                slot = h.slot(-1)
                if i == 0:
                    pe.wait_ge(s_split["o"], h.at(1, 0))
                    pe.wait_ge(s_zlo, h.at(2, -1))
                if i == 4:
                    pe.wait_ge(s_zlo, h.at(2, 0))
                for n, (a, b) in enumerate(((0, 0), (0, 1), (1, 0))):
                    ins = nc.tensor.matmul(accum[ACC_BANK[f"O{i}"]][:, :], zt[:, a, i * P:(i + 1) * P],
                                           w_o[:, slot, b, :], start=(n == 0), stop=(n == 2))
                ins.then_inc(s_o, 1)

            pe.wait_ge(s_ptzero, 1)
            for h in heads_of(pe):
                if h.n < NH - 1 or h.turn is not None:
                    batch = h.at(1, 1) // HEADS
                    base = batch * SEQ if h.turn is None else pe.snap(batch * SEQ)
                for i, step in enumerate(h.steps):
                    for op in step:
                        if op == "S":
                            scores(h, i)
                        elif op in PROJ:
                            pe.wait_ge(s_split[op[0].lower()], h.at(1, 2))
                            acc_free(h, op)
                            project(op, bass.ds(base + int(op[1]) * HALF, HALF), ACC_BANK[op])
                        elif op in ("VA", "VB"):
                            pe.wait_ge(s_projlo, h.at(6, 6 + PROJ["V1" if op == "VB" else "V0"]))
                            tp_free(h, op, 1)
                            v_transpose(op, 1)
                        elif op in ("PV0", "PV1"):
                            acc_free(h, op)
                            values(h, op)
                        elif op == "O":
                            acc_free(h, f"O{i}")
                            output(h, i)
                        else:
                            p_transpose(h, op)

            pe.wait_ge(s_tot, 1)
            nc.tensor.matmul(accum[0][:, 0:3], ones[:, :], totals, start=True, stop=True).then_inc(s_mean, 1)

            def x1_transpose(j, count, free):
                pe.wait_ge(s_x1n, count)
                if free:
                    pe.wait_ge(*free)
                for c in range(C):
                    ins = nc.tensor.transpose(score[(j // 2 + 1) % 2][:, (j % 2) * HALF + c * P:(j % 2) * HALF + (c + 1) * P],
                                              x1n[:, j % 2, c * P:(c + 1) * P], identity[:, :])
                ins.then_inc(s_x1t, 1)

            for j in range(GT):
                x1_transpose(j, j + 1, None)

            def group(g, more):
                at = lambda per, off: g * per + off
                for m in range(MC):
                    if isinstance(g, int) and g == 0 or not isinstance(g, int):
                        pe.wait_ge(s_tern, 2 * m + 2)
                    if m < 2:
                        pe.wait_ge(s_x1lo, at(GT, 4))
                    else:
                        pe.wait_ge(s_gated, at(MC, m - 1))
                    for w, half in ((w1t, 0), (w3t, 1)):
                        for c in range(C):
                            for b in range(2):
                                ins = nc.tensor.matmul(score[m % 2][:, half * HALF:(half + 1) * HALF], w[:, m, c, :],
                                                       x1nt[:, b, c, :], start=(c == 0 and b == 0),
                                                       stop=(c == C - 1 and b == 1))
                    ins.then_inc(s_h, 1)
                if more:
                    for j in range(2):
                        x1_transpose(j, at(GT, GT + j + 1), (s_gated, at(MC, MC - 1)))
                pe.wait_ge(s_tern, 3 * MC)
                for m in range(MC):
                    pe.wait_ge(s_glo, at(MC, m + 1))
                    for j in range(GT):
                        for a in range(2):
                            ins = nc.tensor.matmul(ff_bank(j), gt[:, a, m, j * P:(j + 1) * P], w2t[:, m, :],
                                                   start=(m == 0 and a == 0), stop=(m == MC - 1 and a == 1))
                ins.then_inc(s_f, 1)
                if more:
                    for j in range(2, GT):
                        x1_transpose(j, at(GT, GT + j + 1), (s_gated, at(MC, MC)))

            def ff_bank(j):
                return (tp + accum)[j][:, :]

            with pe.Fori(0, G - 1) as g:
                group(g, True)
            group(G - 1, False)


def kernel(**inputs):
    import numpy as np
    import concourse.bacc as bacc
    from concourse.bass_utils import run_bass_kernel_spmd

    a = {k: np.asarray(val) for k, val in inputs.items()}

    def by_model_dim(w):
        return np.ascontiguousarray(w.reshape(HEADS, E, C, P).transpose(0, 3, 2, 1)).reshape(HEADS, P, C * E)

    def ffn_in(w):
        w = np.pad(w, ((0, MC * P - HIDDEN), (0, 0))).reshape(MC, P, C, P)
        return np.ascontiguousarray(w.transpose(3, 0, 2, 1)).reshape(P, MC, C * P)

    w2 = np.pad(a["L0_ffn_w2"].T, ((0, MC * P - HIDDEN), (0, 0))).reshape(MC, P, D)
    arrays = {
        "x": np.ascontiguousarray(a["L0_attn_x"].reshape(TOK, D)),
        "wq": by_model_dim(a["L0_attn_W_Q"]),
        "wk": by_model_dim(a["L0_attn_W_K"]),
        "wv": by_model_dim(a["L0_attn_W_V"]),
        "wo": np.ascontiguousarray(a["L0_attn_W_O"].transpose(0, 2, 1)),
        "w1": ffn_in(a["L0_ffn_w1"]),
        "w3": ffn_in(a["L0_ffn_w3"]),
        "w2": np.ascontiguousarray(w2.transpose(1, 0, 2)),
    }
    nc = bacc.Bacc("TRN2", target_bir_lowering=False, num_devices=1)
    args = [nc.dram_tensor(name, val.shape, mybir.dt.from_np(val.dtype), kind="ExternalInput").ap()
            for name, val in arrays.items()]
    out = nc.dram_tensor("out", [TOK, D], F32, kind="ExternalOutput").ap()
    block_kernel(nc, *args, out)
    r = run_bass_kernel_spmd(nc, [arrays], core_ids=[0])
    return r.results[0]["out"].reshape(BATCH, SEQ, D)
```

```python
from contextlib import ExitStack

import concourse.bass as bass
from concourse import mybir

ALU = mybir.AluOpType
ACT = mybir.ActivationFunctionType
AX = mybir.AxisListType
F32 = mybir.dt.float32
F32R = mybir.dt.float32r
BF16 = mybir.dt.bfloat16

P = 128
BATCH, SEQ, D = 2, 1024, 512
HEADS, E = 16, 128
HIDDEN = int(2 * D * 4 / 3)
C = D // P
QT = SEQ // P
TOK = BATCH * SEQ
XT = TOK // P
NH = BATCH * HEADS
BODY = 4
TURNS = (NH - BODY) // BODY
HALF = 512
MC = -(-HIDDEN // P)
G = TOK // HALF
GT = HALF // P
QUADS = NH // BODY
SCALE = float(E) ** -0.5
MASKED = -1.0e9 / SCALE
EPS = 1e-5

WIDTH = [256, 256, 384, 512]
FILL = [0, 1, 2, 3, 4, 6, 8, 10]
FILLS = 12

FULL = [["S", "K0", "T7", "O"], ["S", "K1", "PV1", "T0", "O"], ["S", "T1", "V0", "O"], ["S", "T2", "V1", "VA", "O", "T3"],
        ["S", "VB", "O"], ["S", "PV0", "T4", "O"], ["S", "Q0", "T5", "O"], ["S", "Q1", "T6", "O"]]
FIRST = [[op for op in s if op not in ("T7", "PV1", "O")] for s in FULL]
MEANS = [["S", "M"] + FULL[0][1:]] + FULL[1:]
LAST = [[op for op in s if op[0] not in "KVQ"] for s in FULL]
TAIL = [["T7", "O"], ["O"], ["PV1", "O"], ["X0", "O"], ["X1", "O"], ["X2", "O"], ["X3", "O"], ["O"]]
PROJ = {"K0": 1, "K1": 2, "V0": 3, "V1": 4, "Q0": 5, "Q1": 6}
PROJ_HI = {"K0": 1, "K1": 2, "Q0": 3, "Q1": 4}

ACC_BANK = {"K0": 0, "O0": 1, "K1": 0, "PV1": 1, "O1": 0, "V0": 1, "O2": 0, "V1": 1, "O3": 0, "O4": 1,
            "PV0": 0, "O5": 1, "Q0": 0, "O6": 1, "Q1": 0, "O7": 1}
ACC_BEFORE = {"K0": "Q1-", "O0": "O7-", "K1": "K0", "PV1": "O0", "O1": "K1", "V0": "PV1", "O2": "O1", "V1": "V0",
              "O3": "O2", "O4": "V1", "PV0": "O3", "O5": "O4", "Q0": "PV0", "O6": "O5", "Q1": "Q0", "O7": "O6"}
ACC_BEFORE_FIRST = {"K0": "Q1-", "K1": "K0", "V0": "Q1-", "V1": "V0", "PV0": "K1", "Q0": "PV0", "Q1": "Q0"}
ACC_BEFORE_MEANS = {**ACC_BEFORE, "M": "Q1-", "K0": "M"}
ACC_BEFORE_LAST = {**ACC_BEFORE, "O1": "Q1-", "O4": "PV1"}
ACC_BEFORE_TAIL = {"O0": "O7-", "O1": "PV0-", "PV1": "O0", "O2": "O1", "O3": "O2", "O4": "PV1", "O5": "O4",
                   "O6": "O5", "O7": "O6"}
TP_BEFORE = {("T7", 0): ("T6-", 0), ("T7", 1): ("T6-", 1), ("T0", 0): ("T7", 0), ("T1", 1): ("T7", 1),
             ("VA", 1): ("T1", 1), ("T2", 0): ("T0", 0), ("T3", 0): ("T2", 0), ("VB", 1): ("VA", 1),
             ("T4", 0): ("T3", 0), ("T4", 1): ("VB", 1), ("T5", 0): ("T4", 0), ("T5", 1): ("T4", 1),
             ("T6", 0): ("T5", 0), ("T6", 1): ("T5", 1)}
PIECES = 3 * MC
TERNARY = NH - 3
DVE_FIRST, POOL_FIRST = ({2 * j + k: j for j in range(GT)} for k in (0, 1))
DVE_SECOND, POOL_SECOND = ({2 * j + k: j for j in range(GT)} for k in (2, 3))
CHUNK_FIRST, CHUNK_SECOND = ({2 * j + k: j for j in range(GT)} for k in (2, 4))
LATE = (NH - TERNARY) * QT - 1
WEIGH = 8
ONE_BANK = {"T0": 0, "T1": 1, "T2": 0, "T3": 0, "VA": 1, "VB": 1}


class Head:

    def __init__(self, n, turn=None, steps=FULL, before=ACC_BEFORE):
        self.n, self.turn, self.steps, self.before = n, turn, steps, before

    def at(self, per_head, offset):
        fixed = per_head * self.n + offset
        return fixed if self.turn is None else self.turn * (BODY * per_head) + fixed

    def slot(self, n):
        return (self.n + n) % 2


def heads_of(eng):
    yield Head(0, steps=FIRST, before=ACC_BEFORE_FIRST)
    with eng.Fori(0, TURNS) as turn:
        for k in range(BODY):
            yield Head(1 + k, turn)
    yield Head(NH - 3, steps=MEANS, before=ACC_BEFORE_MEANS)
    yield Head(NH - 2)
    yield Head(NH - 1, steps=LAST, before=ACC_BEFORE_LAST)
    yield Head(NH, steps=TAIL, before=ACC_BEFORE_TAIL)


def block_kernel(nc, x, wq, wk, wv, wo, w1, w3, w2, out):
    ctx = ExitStack()
    with ctx:
        def sem(name):
            return ctx.enter_context(nc.semaphore(name))

        R_COLS = 2 * C * TOK + 5 * 2 * C * E + 2 * 2 * SEQ + 2 * SEQ + 2 * 2 * SEQ + 2 * SEQ + 2 * QT * HALF
        F_COLS = 4 * 512 + 2 * SEQ + QT * D + SEQ
        with nc.sbuf_tensor("arena_late", [P, R_COLS], F32) as arena_late:
            pass
        arena_r = ctx.enter_context(nc.sbuf_tensor("arena_r", [P, R_COLS], F32R))
        arena_f = ctx.enter_context(nc.sbuf_tensor("arena_f", [P, F_COLS], F32))
        taken = {"r": 0, "f": 0}
        start = {}

        def f32(ap):
            return ap.bitcast(F32)

        def at_column(which, first, *shape):
            n = 1
            for s in shape:
                n *= s
            assert first + n <= (F_COLS if which == "f" else R_COLS)
            a = {"r": arena_r, "late": arena_late, "f": arena_f}[which][:, first:first + n]
            names = "abcd"[:len(shape)]
            sizes = {names[i]: shape[i] for i in range(1, len(shape))}
            return a.rearrange(f"p ({' '.join(names)}) -> p {' '.join(names)}", **sizes)

        def take(which, name, *shape):
            start[name] = taken[which]
            a = at_column(which, start[name], *shape)
            n = 1
            for s in shape:
                n *= s
            taken[which] += n
            return a

        xnt = take("r", "xnt", BATCH, 2, C * SEQ)
        w_k = take("r", "w_k", 2, C, E)
        w_v = take("r", "w_v", 2, C, E)
        w_q = take("r", "w_q", 2, C, E)
        w_o = take("r", "w_o", 2, 2, C * E)
        kt = take("r", "kt", 2, 2, SEQ)
        qt = take("r", "qt", 2, SEQ)
        v = take("r", "v", 2, 2, QT * E)
        zt = take("r", "zt", 2, SEQ)
        pt = take("r", "pt", 2, QT, HALF)
        raw_k, raw_v, raw_q, raw_o = (take("f", f"raw_{w}", D) for w in "kvqo")
        probs = take("f", "probs", 2, SEQ)
        acc = take("f", "acc", QT, D)
        vt = take("f", "vt", SEQ)
        xin = probs.rearrange("p a (b d) -> p (a b) d", d=D)
        xnt_flat = xnt.rearrange("p a b s -> p (a b s)")
        xnt_by_chunk = xnt.rearrange("p a b (c s) -> p a b c s", c=C)
        weigh = acc

        w13t = at_column("r", 0, MC, 2, C, P)
        w2t = at_column("r", MC * 2 * D, MC, D)
        w2t_end = MC * 3 * D
        assert w2t_end <= start["w_v"]
        extra = ctx.enter_context(nc.sbuf_tensor("extra", [P, 6 * D], F32)).rearrange("p (a b) -> p a b", b=D)
        is_less = [extra[:, 0, :], extra[:, 1, :]]
        wraw = [extra[:, 2, :], extra[:, 3, :]]
        stage = [extra[:, 4:6, :], at_column("late", start["w_v"], 2, D)]
        x1_next = at_column("late", start["kt"], GT, D)
        x1n = at_column("late", start["v"], GT, D)
        x1nt = at_column("r", start["pt"], 2, C, HALF)
        spare = [first + k * HALF for first, last in ((start["kt"] + 2 * SEQ, start["v"]),
                                                      (start["v"] + 2 * SEQ, start["pt"]),
                                                      (start["pt"] + 2 * C * HALF, R_COLS))
                 for k in range((last - first) // HALF)]
        gt = [[at_column("r", spare[2 * m + a], HALF) for m in range(MC)] for a in range(2)]
        x1_now = at_column("f", start["probs"], GT, D)
        fin = at_column("f", start["acc"], GT, D)
        gate = raw_o
        ghid = at_column("f", start["vt"], D)

        small = ctx.enter_context(nc.sbuf_tensor("small", [P, 176], F32))
        negmax, rowsum, rinv = small[:, 0:8], small[:, 8:16], small[:, 16:24]
        stats = small[:, 24:36].rearrange("p (a b) -> p a b", b=6)
        mv = small[:, 36:40].rearrange("p (a b) -> p a b", b=2)
        varp = small[:, 40:42]
        rstd = small[:, 42:44]
        power = small[:, 44:45]
        totals = small[:, 48:51]
        scales = small[:, 51:54]
        above = small[:, 54:57]
        below = small[:, 57:60]
        squared = small[:, 71:72]
        abssum = small[:, 80:80 + PIECES]
        mv3 = small[:, 116:124].rearrange("p (a b) -> p a b", b=2)
        scaled3 = small[:, 124:128]
        rstd3 = small[:, 128:132]
        factor3 = small[:, 132:136]
        shift3 = small[:, 136:140]
        stats3 = small[:, 150:174].rearrange("p (a b) -> p a b", b=6)
        keep = small[:, 140:140 + TURNS]
        identity = ctx.enter_context(nc.sbuf_tensor("identity", [P, P], F32))
        ones = ctx.enter_context(nc.sbuf_tensor("ones", [P, P], F32))
        identity_b = ctx.enter_context(nc.sbuf_tensor("identity_b", [P, P], BF16))
        mask = ctx.enter_context(nc.sbuf_tensor("mask", [P, P], BF16))

        score = [ctx.enter_context(nc.psum_tensor(f"score{i}", [P, SEQ], F32)) for i in range(2)]
        tp = [ctx.enter_context(nc.psum_tensor(f"tp{i}", [P, HALF], F32)) for i in range(2)]
        accum = [ctx.enter_context(nc.psum_tensor(f"accum{i}", [P, HALF], F32)) for i in range(2)]

        running = nc.dram_tensor("running", [BATCH, P, QT, D], F32, kind="Internal").ap()

        s_const = sem("s_const")
        s_mask = sem("s_mask")
        s_xin = [sem(f"s_xin{i}") for i in range(4)]
        s_bn, s_var = sem("s_bn"), sem("s_var")
        s_eps, s_rstd = sem("s_eps"), sem("s_rstd")
        s_xn = sem("s_xn")
        s_xt, s_xhi, s_xlo = sem("s_xt"), sem("s_xhi"), sem("s_xlo")
        s_raw = {w: sem(f"s_raw_{w}") for w in "kvqo"}
        s_split_hi = {w: sem(f"s_split_hi_{w}") for w in "kvqo"}
        s_split = {w: sem(f"s_split_{w}") for w in "kvqo"}
        s_proj, s_projhi, s_projlo = sem("s_proj"), sem("s_projhi"), sem("s_projlo")
        s_vt, s_vhi, s_vlo = sem("s_vt"), sem("s_vhi"), sem("s_vlo")
        s_score, s_negmax, s_exp = sem("s_score"), sem("s_negmax"), sem("s_exp")
        s_rinv, s_norm = sem("s_rinv"), sem("s_norm")
        s_t, s_thi, s_tlo = sem("s_t"), sem("s_thi"), sem("s_tlo")
        s_pv, s_zhi, s_zlo = sem("s_pv"), sem("s_zhi"), sem("s_zlo")
        s_o = sem("s_o")
        s_sum = sem("s_sum")
        s_part = sem("s_part")
        s_accfree = sem("s_accfree")
        s_passed = [sem("s_passed_pool"), sem("s_passed_dve")]
        s_ptzero = sem("s_ptzero")
        s_weigh = [sem(f"s_weigh{i}") for i in range(WEIGH)]
        s_acczero = sem("s_acczero")
        s_w = [sem(f"s_w{i}") for i in range(2)]
        s_abs = sem("s_abs")
        s_tot, s_mean, s_thr = sem("s_tot"), sem("s_mean"), sem("s_thr")
        s_less, s_tern = sem("s_less"), sem("s_tern")
        s_stage = [sem(f"s_stage{i}") for i in range(2)]
        s_fbn, s_fvar, s_feps, s_frstd = sem("s_fbn"), sem("s_fvar"), sem("s_feps"), sem("s_frstd")
        s_y, s_x1 = sem("s_y"), sem("s_x1")
        s_x1n, s_x1t = sem("s_x1n"), sem("s_x1t")
        s_x1hi, s_x1lo = sem("s_x1hi"), sem("s_x1lo")
        s_now = sem("s_now")
        s_h, s_silu, s_gated, s_ghi, s_glo = (sem(f"s_{n}") for n in ("h", "silu", "gated", "ghi", "glo"))
        s_f = sem("s_f")
        s_obn, s_ovar, s_oeps, s_orstd = sem("s_obn"), sem("s_ovar"), sem("s_oeps"), sem("s_orstd")
        s_oscale = sem("s_oscale")
        s_oshift, s_onorm, s_fin, s_out = sem("s_oshift"), sem("s_onorm"), sem("s_fin"), sem("s_out")

        block = ctx.enter_context(nc.Block())

        def fill(h, i, second=False):
            return h.at(FILLS, FILL[i] + 1 + second)

        def key_slot(group, j):
            return QT - 1 if j == 4 * group + 3 else j

        def alone(eng, which):
            eng.sem_inc(s_passed[which], 1)

        def tile_of(op):
            return int(op[1:])

        def fills_of(op):
            if op in ONE_BANK:
                return [(ONE_BANK[op], 0, 4 if op[0] == "V" else tile_of(op) + 1)]
            return [(0, 0, 4), (1, 4, tile_of(op) - 3)]

        def pt_block(hilo, i, j0, n):
            q = slice(i % 4 * P, (i % 4 + 1) * P)
            js = list(range(j0, j0 + n))
            last = 4 * (i // 4) + 3
            runs = []
            if last in js and key_slot(i // 4, last) != last:
                js.remove(last)
                runs = [(last - j0, 1, pt[:, hilo, QT - 1:QT, q])]
            return [(js[0] - j0, len(js), pt[:, hilo, js[0]:js[0] + len(js), q])] + runs

        def x_columns(batch, hilo, c, first, n):
            return bass.ds(batch * (2 * C * SEQ) + ((hilo * C + c) * SEQ + first), n)

        def ternary_place(n):
            if n < 2 * MC:
                return w13t[:, n // 2, n % 2, :, :].rearrange("p c h -> p (c h)")
            return w2t[:, n - 2 * MC, :]

        def weight_of(n):
            return (n % 2, n // 2) if n < 2 * MC else (2, n - 2 * MC)

        def ternary_in_head(n, i, lag):
            k = (n - TERNARY) * QT + i - 1 - lag
            return [k] if 0 <= k < LATE else []

        def ternary_in_group(m, lag):
            k = LATE + m - lag
            return [k] if LATE <= k < PIECES else []

        def x1_bank(j):
            return score[(j // 2 + 1) % 2][:, j % 2 * HALF:(j % 2 + 1) * HALF]

        def ff_bank(j):
            return (tp + accum)[j][:, :]

        @block.sync
        def _(sp):
            def load(w, src, head):
                dst = {"k": raw_k, "v": raw_v, "q": raw_q, "o": raw_o}[w]
                sp.dma_start(dst, src[head]).then_inc(s_raw[w], 16)

            def load_weight(n):
                which, m = weight_of(n)
                if n >= 2:
                    sp.wait_ge(s_tern, n - 1)
                sp.dma_start(wraw[n % 2], (w1, w3, w2)[which][:, m, :]).then_inc(s_w[n % 2], 16)

            def loads_at(n, i):
                k = (n - TERNARY) * QT + i
                return (0, 1) if k == 0 else () if k == 1 else (k - 1, k) if i == 0 else (k,)

            def load_tile(g, j):
                if j >= 2:
                    sp.wait_ge(s_x1, g * GT + (GT + j - 1))
                b, half = (g + 1) // 2, (g + 1) % 2
                sp.dma_start(stage[j % 2][:, 0:1, :], running[bass.ds(b, 1), :, bass.ds(half * 4 + j, 1), :]
                             .rearrange("q p a d -> p q (a d)")).then_inc(s_stage[j % 2], 16)
                sp.dma_start(stage[j % 2][:, 1, :], x[bass.ds(g * HALF + (HALF + j * P), P), :]
                             ).then_inc(s_stage[j % 2], 16)

            def load_x(n):
                if n >= 4:
                    sp.wait_ge(s_xt, n - 3)
                sp.dma_start(xin[:, n % 4, :], x[n * P:(n + 1) * P, :]).then_inc(s_xin[n % 4], 16)

            for n in range(4):
                load_x(n)
            load("k", wk, 0)
            load("v", wv, 0)
            load("q", wq, 0)
            load("o", wo, 0)
            for n in range(4, 12):
                load_x(n)
            sp.wait_ge(s_split["k"], 1)
            load("k", wk, 1)
            sp.wait_ge(s_split["v"], 1)
            load("v", wv, 1)
            load_x(12)
            load_x(13)
            sp.wait_ge(s_split["q"], 1)
            load("q", wq, 1)
            load_x(14)
            load_x(15)
            sp.wait_ge(s_split["k"], 2)
            load("k", wk, 2)
            sp.wait_ge(s_split["v"], 2)
            load("v", wv, 2)
            sp.sem_inc(s_accfree, 1)
            for h in heads_of(sp):
                last = h.turn is None
                if not (last and h.n + 2 > NH - 1):
                    sp.wait_ge(s_split["q"], h.at(1, 2))
                    load("q", wq, h.at(1, 2) % HEADS)
                if not (last and h.n + 3 > NH - 1):
                    sp.wait_ge(s_split["k"], h.at(1, 3))
                    load("k", wk, h.at(1, 3) % HEADS)
                    sp.wait_ge(s_split["v"], h.at(1, 3))
                    load("v", wv, h.at(1, 3) % HEADS)
                if h.n % BODY == 0 and not (last and h.n == 0):
                    quad = h.turn if h.turn is not None else QUADS - 1
                    b = bass.ds(h.turn // (HEADS // BODY), 1) if h.turn is not None else bass.ds(BATCH - 1, 1)
                    sp.wait_ge(s_sum, h.at(QT, 4))
                    sp.dma_start(running[b, :, 0:4, :].rearrange("b p i d -> p (b i) d"), acc[:, 0:4, :]
                                 ).then_inc(s_part, 16)
                if last and h.n >= TERNARY and h.n < NH:
                    for i in range(QT if h.n == NH - 1 else QT - 1):
                        for n in loads_at(h.n, i):
                            load_weight(n)
                        if h.n == NH - 3 and i == 0:
                            load_tile(-1, 0)
                        if h.n == NH - 2 and i == 3:
                            sp.wait_ge(s_proj, 6 * (NH - 1) + PROJ["V1"])
                            load_tile(-1, 1)
                        if h.n == NH - 1 and i in (2, 4):
                            load_tile(-1, i // 2 + 1)
                if not (last and h.n + 1 > NH - 1):
                    sp.wait_ge(s_split["o"], h.at(1, 1))
                    load("o", wo, h.at(1, 1) % HEADS)
                if h.n % BODY == 0 and not (last and h.n == 0):
                    sp.wait_ge(s_sum, h.at(QT, 8))
                    sp.dma_start(running[b, :, 4:8, :].rearrange("b p i d -> p (b i) d"), acc[:, 4:8, :]
                                 ).then_inc(s_part, 16)
                    sp.wait_ge(s_part, 32 * (quad + 1) if last else h.turn * 32 + 32)
                    sp.sem_inc(s_accfree, 1)

            def store(g):
                for j in range(GT):
                    sp.wait_ge(s_fin, g * GT + (j + 1))
                    sp.dma_start(out[bass.ds(g * HALF + j * P, P), :], fin[:, j, :]).then_inc(s_out, 16)

            load_tile(0, 0)
            load_tile(0, 1)
            tiles = {LATE + 5: 2, LATE + 7: 3}
            for n in range(LATE + 1, PIECES):
                load_weight(n)
                if n in tiles:
                    load_tile(0, tiles[n])
            store(0)
            with sp.Fori(1, G - 1) as g:
                for j in range(GT):
                    load_tile(g, j)
                store(g)
            store(G - 1)
            sp.wait_ge(s_out, 16 * G * GT)

        @block.gpsimd
        def _(pool):
            nc.gpsimd.memset(identity[:, :], 0.0).then_inc(s_mask, 1)
            nc.gpsimd.memset(mask[:, :], 0.0).then_inc(s_mask, 1)
            nc.gpsimd.memset(identity_b[:, :], 0.0).then_inc(s_mask, 1)
            nc.gpsimd.memset(power, -0.5).then_inc(s_mask, 1)
            for turn in range(TURNS):
                nc.gpsimd.memset(keep[:, turn:turn + 1], 0.0 if turn * BODY % HEADS == 0 else 1.0).then_inc(s_mask, 1)
            nc.gpsimd.memset(ones[:, :], 1.0).then_inc(s_const, 1)
            pool.wait_ge(s_mask, 4 + TURNS)
            for m in (identity, identity_b):
                nc.gpsimd.affine_select(out=m[:, :], in_=m[:, :], compare_op=ALU.not_equal, fill=1.0, base=0,
                                        pattern=[[-1, P]], channel_multiplier=1).then_inc(s_const, 1)
            nc.gpsimd.affine_select(out=mask[:, :], in_=mask[:, :], compare_op=ALU.is_ge, fill=MASKED, base=0,
                                    pattern=[[-1, P]], channel_multiplier=1).then_inc(s_const, 1)

            def rsqrt(n):
                pool.wait_ge(s_var, n + 1)
                nc.gpsimd.tensor_scalar(varp[:, n % 2:n % 2 + 1], mv[:, n % 2, 1:2], EPS, None, ALU.add
                                        ).then_inc(s_eps, 1)
                pool.wait_ge(s_eps, n + 1)
                nc.gpsimd.tensor_tensor(rstd[:, n % 2:n % 2 + 1], varp[:, n % 2:n % 2 + 1], power, ALU.pow
                                        ).then_inc(s_rstd, 1)

            def split(w, raw_count, count):
                raw = {"k": raw_k, "v": raw_v, "q": raw_q, "o": raw_o}[w[0]]
                dst = {"k": w_k, "v": w_v, "q": w_q}.get(w[0])
                hi, lo = ((w_o[:, w[1], p, :] for p in range(2)) if dst is None
                          else (dst[:, p, :, :].rearrange("p c e -> p (c e)") for p in range(2)))
                pool.wait_ge(s_raw[w[0]], raw_count)
                alone(pool, 0)
                nc.gpsimd.tensor_copy(hi, raw).then_inc(s_split_hi[w[0]], 1)
                pool.wait_ge(s_split_hi[w[0]], count)
                nc.gpsimd.tensor_tensor(lo, raw, f32(hi), ALU.subtract).then_inc(s_split[w[0]], 1)

            for n in range(8):
                rsqrt(n)
                if n == 2:
                    split("k", 16, 1)
                if n == 4:
                    split("v", 16, 1)
                if n == 6:
                    split("q", 16, 1)
            for n in range(8, XT):
                rsqrt(n)
            pool.wait_ge(s_proj, 2)
            split("k", 32, 2)
            pool.wait_ge(s_proj, 4)
            split("v", 32, 2)

            def less(n):
                if n == 0:
                    pool.wait_ge(s_thr, 4)
                pool.wait_ge(s_w[n % 2], 16 * (n // 2 + 1))
                if n >= 2:
                    pool.wait_ge(s_tern, n - 1)
                w = weight_of(n)[0]
                nc.gpsimd.tensor_scalar(is_less[n % 2], wraw[n % 2], below[:, w:w + 1], None, ALU.is_lt
                                        ).then_inc(s_less, 1)

            def tile_rsqrt(k, count):
                pool.wait_ge(s_fvar, count)
                alone(pool, 0)
                nc.gpsimd.tensor_scalar(varp[:, k:k + 1], mv[:, k, 1:2], EPS, None, ALU.add).then_inc(s_feps, 1)
                pool.wait_ge(s_feps, count)
                nc.gpsimd.tensor_tensor(rstd[:, k:k + 1], varp[:, k:k + 1], power, ALU.pow).then_inc(s_frstd, 1)
                pool.wait_ge(s_frstd, count)
                alone(pool, 0)

            def first_step(g, j):
                at = lambda per, off: g * (per * GT) + (per * (GT + j) + off)
                tile_rsqrt(0, at(2, 1))
                nc.gpsimd.tensor_scalar(stage[j % 2][:, 0, :], stage[j % 2][:, 0, :], mv[:, 0, 0:1], rstd[:, 0:1],
                                        ALU.subtract, ALU.mult).then_inc(s_y, 1)
                pool.wait_ge(s_y, at(1, 1))
                if j == 0 and not (isinstance(g, int) and g < 0):
                    pool.wait_ge(s_now, g + 1)
                nc.gpsimd.tensor_tensor(x1_next[:, j, :], stage[j % 2][:, 0, :], stage[j % 2][:, 1, :], ALU.add
                                        ).then_inc(s_x1, 1)

            def second_step(g, j):
                at = lambda per, off: g * (per * GT) + (per * (GT + j) + off)
                if isinstance(g, int) and g < 0:
                    pool.wait_ge(s_pv, 2 * (NH - 1))
                else:
                    pool.wait_ge(s_x1t, at(1, 1 - GT))
                tile_rsqrt(1, at(2, 2))
                nc.gpsimd.tensor_scalar(x1n[:, j, :], x1_next[:, j, :], mv[:, 1, 0:1], rstd[:, 1:2],
                                        ALU.subtract, ALU.mult).then_inc(s_x1n, 1)

            for h in heads_of(pool):
                if h.n == NH:
                    for i in range(QT, 2 * QT):
                        if i in POOL_SECOND:
                            second_step(-1, POOL_SECOND[i])
                    break
                fixed = h.turn is None
                for i in range(QT):
                    pool.wait_ge(s_rinv, h.at(QT, i + 1))
                    alone(pool, 0)
                    pr = probs[:, i % 2, 0:(i + 1) * P]
                    nc.gpsimd.tensor_scalar(pr, pr, rinv[:, i:i + 1], 1.0, ALU.mult, ALU.mult).then_inc(s_norm, 1)
                    if i == 0 and not (fixed and h.n + 1 > NH - 1):
                        pool.wait_ge(s_proj, h.at(6, 6))
                        split("q", h.at(16, 32), h.at(1, 2))
                    if i == 2 and not (fixed and h.n + 2 > NH - 1):
                        pool.wait_ge(s_proj, h.at(6, 8))
                        split("k", h.at(16, 48), h.at(1, 3))
                    if i == 4 and not (fixed and h.n + 2 > NH - 1):
                        pool.wait_ge(s_proj, h.at(6, 10))
                        split("v", h.at(16, 48), h.at(1, 3))
                    if i == 6:
                        split(("o", h.slot(0)), h.at(16, 16), h.at(1, 1))
                    if fixed and h.n >= TERNARY:
                        for n in ternary_in_head(h.n, i, 0):
                            less(n)
                    if fixed and h.n == NH - 1:
                        if i in POOL_SECOND:
                            second_step(-1, POOL_SECOND[i])
                        if i in POOL_FIRST:
                            first_step(-1, POOL_FIRST[i])
                if fixed and h.n == 0:
                    pool.wait_ge(s_abs, PIECES)
                    nc.gpsimd.memset(acc[:, :, :], 0.0).then_inc(s_acczero, 1)

            def finish(g):
                def scale_tile(j):
                    at = g * GT + (j + 1)
                    col = slice(j, j + 1)
                    pool.wait_ge(s_ovar, at)
                    alone(pool, 0)
                    nc.gpsimd.tensor_scalar(scaled3[:, col], mv3[:, j, 1:2], squared, EPS, ALU.mult, ALU.add
                                            ).then_inc(s_oeps, 1)
                    pool.wait_ge(s_oeps, at)
                    nc.gpsimd.tensor_tensor(rstd3[:, col], scaled3[:, col], power, ALU.pow).then_inc(s_orstd, 1)
                    pool.wait_ge(s_orstd, at)
                    nc.gpsimd.tensor_tensor(factor3[:, col], rstd3[:, col], scales[:, 2:3], ALU.mult
                                            ).then_inc(s_oscale, 1)
                    pool.wait_ge(s_oscale, at)
                    alone(pool, 0)
                    nc.gpsimd.tensor_scalar(shift3[:, col], mv3[:, j, 0:1], factor3[:, col], -1.0, ALU.mult, ALU.mult
                                            ).then_inc(s_oshift, 1)

                def add_tile(j):
                    pool.wait_ge(s_onorm, g * GT + (j + 1))
                    nc.gpsimd.tensor_tensor(fin[:, j, :], fin[:, j, :], x1_now[:, j, :], ALU.add).then_inc(s_fin, 1)

                for j in range(GT):
                    scale_tile(j)
                    if j:
                        add_tile(j - 1)
                add_tile(GT - 1)

            def group(g, first, more):
                for m in range(MC):
                    if first:
                        for n in ternary_in_group(m, 0):
                            less(n)
                    if more and m in CHUNK_SECOND:
                        second_step(g, CHUNK_SECOND[m])
                    if more and m in CHUNK_FIRST:
                        first_step(g, CHUNK_FIRST[m])
                finish(g)

            group(0, True, True)
            with pool.Fori(1, G - 1) as g:
                group(g, False, True)
            group(G - 1, False, False)

        @block.scalar
        def _(act):
            def x_hi(n):
                act.wait_ge(s_xt, n + 1)
                nc.scalar.activation(xnt_by_chunk[:, n // QT, 0, :, n % QT * P:(n % QT + 1) * P], tp[n % 2][:, :].rearrange("p (c q) -> p c q", c=C),
                                     ACT.Copy).then_inc(s_xhi, 1)

            def proj_hi(op, slot, count, hi_count, bank):
                half = slice(int(op[1]) * HALF, (int(op[1]) + 1) * HALF)
                act.wait_ge(s_proj, count)
                dst = kt[:, slot, 0, half] if op[0] == "K" else qt[:, 0, half]
                nc.scalar.activation(dst, accum[bank][:, :], ACT.Copy, scale=1.0 if op[0] == "K" else SCALE
                                     ).then_inc(s_projhi, 1)

            def v_hi(op, slot, count, bank):
                half = slice(HALF * (op == "VB"), HALF * (op == "VB") + HALF)
                act.wait_ge(s_vt, count)
                nc.scalar.activation(v[:, slot, 0, half], tp[bank][:, :], ACT.Copy).then_inc(s_vhi, 1)

            pieces = iter(range(PIECES))

            def load_to_weigh(n):
                which, m = (n // MC, n % MC)
                if n >= WEIGH:
                    act.wait_ge(s_abs, n - WEIGH + 1)
                act.dma_start(weigh[:, n % WEIGH, :], (w1, w3, w2)[which][:, m, :]).then_inc(s_weigh[n % WEIGH], 16)

            def weigh_next(count):
                for _, n in zip(range(count), pieces):
                    act.wait_ge(s_weigh[n % WEIGH], 16 * (n // WEIGH + 1))
                    nc.scalar.activation(weigh[:, n % WEIGH, :], weigh[:, n % WEIGH, :], ACT.Abs,
                                         accum_out=abssum[:, n:n + 1]).then_inc(s_abs, 1)
                    if WEIGH <= n + WEIGH - 1 < PIECES and n:
                        load_to_weigh(n + WEIGH - 1)

            for n in range(8):
                x_hi(n)
                if n == 3:
                    for k in range(WEIGH):
                        load_to_weigh(k)
            for n, op in enumerate(("K0", "K1")):
                proj_hi(op, 0, PROJ[op], PROJ_HI[op], n % 2)
                weigh_next(1)
            for n in range(8, 12):
                x_hi(n)
                weigh_next(1)
            v_hi("VA", 0, 1, 0)
            v_hi("VB", 0, 2, 1)
            weigh_next(1)
            for n, op in enumerate(("Q0", "Q1")):
                proj_hi(op, 0, PROJ[op], PROJ_HI[op], n % 2)
                weigh_next(1)
            for n in range(12, XT):
                x_hi(n)
                weigh_next(1)

            def x1_hi(j, bank, count):
                act.wait_ge(s_x1t, count)
                nc.scalar.activation(x1nt[:, 0, :, j * P:(j + 1) * P], bank.rearrange("p (c q) -> p c q", c=C), ACT.Copy
                                     ).then_inc(s_x1hi, 1)

            for h in heads_of(act):
                for i, step in enumerate(h.steps):
                    if "S" in step:
                        act.wait_ge(s_negmax, h.at(QT, i + 1))
                        if i >= 2 or h.n > 0:
                            before = fill(h, i - 2, i - 2 >= 4) if i >= 2 else h.at(FILLS, (-2, 0)[i])
                            act.wait_ge(s_t, before)
                        nc.scalar.activation(probs[:, i % 2, 0:(i + 1) * P], score[i % 2][:, 0:(i + 1) * P], ACT.Exp,
                                             bias=negmax[:, i:i + 1], scale=1.0,
                                             accum_out=rowsum[:, i:i + 1]).then_inc(s_exp, 1)
                    for op in step:
                        if op in PROJ_HI:
                            proj_hi(op, h.slot(1), h.at(6, 6 + PROJ[op]), None, ACC_BANK[op])
                        elif op in ("VA", "VB"):
                            v_hi(op, h.slot(1), h.at(2, 3 + (op == "VB")), 1)
                        elif op in ("PV0", "PV1"):
                            half = slice(int(op[2]) * HALF, (int(op[2]) + 1) * HALF)
                            act.wait_ge(s_pv, h.at(2, 1 if op == "PV0" else 0))
                            nc.scalar.activation(zt[:, 0, half], accum[ACC_BANK[op]][:, :], ACT.Copy).then_inc(s_zhi, 1)
                        elif op[0] == "T":
                            q = tile_of(op)
                            if q == 0 and h.n > 0:
                                act.wait_ge(s_pv, h.at(2, 0))
                            if q == 4:
                                act.wait_ge(s_pv, h.at(2, 1))
                            for f, (bank, j0, n) in enumerate(fills_of(op)):
                                act.wait_ge(s_t, h.at(FILLS, FILL[q] + 1 + f - (FILLS if q == 7 else 0)))
                                src = tp[bank][:, 0:n * P].rearrange("p (j q) -> p j q", q=P)
                                for k, (at, m, dst) in enumerate(pt_block(0, q, j0, n)):
                                    ins = nc.scalar.activation(dst, src[:, at:at + m, :], ACT.Copy)
                                ins.then_inc(s_thi, 1)
                        elif op[0] == "X":
                            x1_hi(tile_of(op), tp[tile_of(op) % 2][:, :], tile_of(op) + 1)
                    if h.n == 0:
                        weigh_next(3)

            def group(g, first, more):
                at = lambda per, off: g * per + off
                for m in range(MC):
                    act.wait_ge(s_h, at(MC, m + 1))
                    nc.scalar.activation(gate, score[m % 2][:, 0:HALF], ACT.Silu, scale=scales[:, 0:1]).then_inc(s_silu, 1)
                    act.wait_ge(s_gated, at(MC, m + 1))
                    nc.scalar.activation(gt[0][m], ghid, ACT.Copy).then_inc(s_ghi, 1)
                    if m == 0:
                        act.wait_ge(s_x1n, at(GT, GT))
                        if not first:
                            act.wait_ge(s_fin, at(GT, 0))
                        nc.scalar.activation(x1_now, x1_next, ACT.Copy).then_inc(s_now, 1)

                def normalise(j):
                    act.wait_ge(s_oshift, at(GT, j + 1))
                    if first:
                        act.wait_ge(s_part, 32 * QUADS)
                    else:
                        act.wait_ge(s_out, at(GT * 16, 0))
                    nc.scalar.activation(fin[:, j, :], ff_bank(j), ACT.Identity, bias=shift3[:, j:j + 1],
                                         scale=factor3[:, j:j + 1]).then_inc(s_onorm, 1)

                for j in range(GT):
                    if more and j < 2:
                        for k in (2 * j, 2 * j + 1):
                            x1_hi(k, x1_bank(k), at(GT, GT + k + 1))
                    normalise(j)

            group(0, True, True)
            with act.Fori(1, G - 1) as g:
                group(g, False, True)
            group(G - 1, False, False)

        @block.vector
        def _(dve):
            nc.vector.memset(f32(pt[:, :, QT - 1, 2 * P:3 * P]), 0.0).then_inc(s_ptzero, 1)
            dve.sem_inc(s_sum, QT)

            def x_stats(n):
                dve.wait_ge(s_xin[n % 4], 16 * (n // 4 + 1))
                nc.vector.bn_stats(stats[:, n % 2, :], xin[:, n % 4, :]).then_inc(s_bn, 1)
                dve.wait_ge(s_bn, n + 1)
                nc.vector.bn_aggr(mv[:, n % 2, :], stats[:, n % 2, :]).then_inc(s_var, 1)

            def x_norm(n):
                dve.wait_ge(s_rstd, n + 1)
                nc.vector.tensor_scalar(xin[:, n % 4, :], xin[:, n % 4, :], mv[:, n % 2, 0:1],
                                        rstd[:, n % 2:n % 2 + 1], ALU.subtract, ALU.mult).then_inc(s_xn, 1)

            def x_lo(n):
                dve.wait_ge(s_xhi, n + 1)
                cols = slice(n % QT * P, (n % QT + 1) * P)
                nc.vector.tensor_tensor(xnt_by_chunk[:, n // QT, 1, :, cols],
                                        tp[n % 2][:, :].rearrange("p (c q) -> p c q", c=C),
                                        f32(xnt_by_chunk[:, n // QT, 0, :, cols]), ALU.subtract).then_inc(s_xlo, 1)

            def proj_lo(op, slot, count, hi_count, bank):
                half = slice(int(op[1]) * HALF, (int(op[1]) + 1) * HALF)
                if op[0] == "V":
                    dve.wait_ge(s_proj, count)
                    nc.vector.tensor_copy(vt[:, half], accum[bank][:, :]).then_inc(s_projlo, 1)
                    return
                dve.wait_ge(s_projhi, hi_count)
                if op[0] == "K":
                    nc.vector.tensor_tensor(kt[:, slot, 1, half], accum[bank][:, :], f32(kt[:, slot, 0, half]),
                                            ALU.subtract).then_inc(s_projlo, 1)
                else:
                    nc.vector.scalar_tensor_tensor(qt[:, 1, half], accum[bank][:, :], SCALE, f32(qt[:, 0, half]),
                                                   ALU.mult, ALU.subtract).then_inc(s_projlo, 1)

            def v_lo(op, slot, count, bank):
                half = slice(HALF * (op == "VB"), HALF * (op == "VB") + HALF)
                dve.wait_ge(s_vhi, count)
                nc.vector.tensor_tensor(v[:, slot, 1, half], tp[bank][:, :], f32(v[:, slot, 0, half]),
                                        ALU.subtract).then_inc(s_vlo, 1)

            x_stats(0)
            x_stats(1)
            for n in range(8):
                x_norm(n)
                if n < 6:
                    x_stats(n + 2)
                if n:
                    x_lo(n - 1)
            x_lo(7)
            x_stats(8)
            x_stats(9)
            for n, op in enumerate(("K0", "K1", "V0", "V1")):
                proj_lo(op, 0, PROJ[op], PROJ_HI.get(op), n % 2)
                x_norm(8 + n)
                x_stats(10 + n)
            for n in range(8, 12):
                x_lo(n)
            v_lo("VA", 0, 1, 0)
            v_lo("VB", 0, 2, 1)
            for n, op in enumerate(("Q0", "Q1")):
                proj_lo(op, 0, PROJ[op], PROJ_HI[op], n % 2)
                x_norm(12 + n)
                x_stats(14 + n)
            x_norm(14)
            x_norm(15)
            for n in range(12, XT):
                x_lo(n)

            def add_out(h, i):
                dve.wait_ge(s_o, h.at(QT, i + 1 - QT))
                if (h.n - 1) % BODY == 0 and i == 0:
                    dve.wait_ge(s_accfree, h.turn + 1 if h.turn is not None else QUADS)
                if h.turn is not None and h.n == 1:
                    nc.vector.scalar_tensor_tensor(acc[:, i, :], acc[:, i, :], keep[:, bass.ds(h.turn, 1)],
                                                   accum[ACC_BANK[f"O{i}"]][:, :], ALU.mult, ALU.add).then_inc(s_sum, 1)
                else:
                    nc.vector.tensor_tensor(acc[:, i, :], accum[ACC_BANK[f"O{i}"]][:, :], acc[:, i, :], ALU.add
                                            ).then_inc(s_sum, 1)

            def ternary(n):
                dve.wait_ge(s_less, n + 1)
                w = weight_of(n)[0]
                nc.vector.scalar_tensor_tensor(ternary_place(n), wraw[n % 2], above[:, w:w + 1], is_less[n % 2],
                                               ALU.is_gt, ALU.subtract).then_inc(s_tern, 1)

            def statistics(k, src, count):
                nc.vector.bn_stats(stats[:, k, :], src).then_inc(s_fbn, 1)
                dve.wait_ge(s_fbn, count)
                alone(dve, 1)
                nc.vector.bn_aggr(mv[:, k, :], stats[:, k, :]).then_inc(s_fvar, 1)

            def first_stats(g, j):
                dve.wait_ge(s_stage[j % 2], g * 64 + (64 + 32 + 32 * (j // 2)))
                statistics(0, stage[j % 2][:, 0, :], g * (2 * GT) + (2 * (GT + j) + 1))

            def second_stats(g, j):
                dve.wait_ge(s_x1, g * GT + (GT + j + 1))
                if j or not isinstance(g, int) or g >= 0:
                    dve.wait_ge(s_x1n, g * GT + (GT + j))
                statistics(1, x1_next[:, j, :], g * (2 * GT) + (2 * (GT + j) + 2))

            def x1_lo(j, bank, count):
                dve.wait_ge(s_x1hi, count)
                cols = slice(j * P, (j + 1) * P)
                nc.vector.tensor_tensor(x1nt[:, 1, :, cols], bank.rearrange("p (c q) -> p c q", c=C),
                                        f32(x1nt[:, 0, :, cols]), ALU.subtract).then_inc(s_x1lo, 1)

            for h in heads_of(dve):
                for i, step in enumerate(h.steps):
                    if "S" in step:
                        dve.wait_ge(s_score, h.at(QT, i + 1))
                        nc.vector.tensor_reduce(negmax[:, i:i + 1], score[i % 2][:, 0:(i + 1) * P], AX.X, ALU.max,
                                                negate=True).then_inc(s_negmax, 1)
                    if i > 0 and "O" in h.steps[i - 1]:
                        add_out(h, i - 1)
                    if "S" in step:
                        dve.wait_ge(s_exp, h.at(QT, i + 1))
                        nc.vector.reciprocal(rinv[:, i:i + 1], rowsum[:, i:i + 1]).then_inc(s_rinv, 1)
                    for op in step:
                        if op in PROJ:
                            proj_lo(op, h.slot(1), h.at(6, 6 + PROJ[op]),
                                    h.at(4, 4 + PROJ_HI[op]) if op in PROJ_HI else None, ACC_BANK[op])
                        elif op in ("VA", "VB"):
                            v_lo(op, h.slot(1), h.at(2, 3 + (op == "VB")), 1)
                        elif op in ("PV0", "PV1"):
                            half = slice(int(op[2]) * HALF, (int(op[2]) + 1) * HALF)
                            dve.wait_ge(s_zhi, h.at(2, 1 if op == "PV0" else 0))
                            nc.vector.tensor_tensor(zt[:, 1, half], accum[ACC_BANK[op]][:, :], f32(zt[:, 0, half]),
                                                    ALU.subtract).then_inc(s_zlo, 1)
                        elif op[0] == "T":
                            q = tile_of(op)
                            for f, (bank, j0, n) in enumerate(fills_of(op)):
                                dve.wait_ge(s_thi, h.at(FILLS, FILL[q] + 1 + f - (FILLS if q == 7 else 0)))
                                src = tp[bank][:, 0:n * P].rearrange("p (j q) -> p j q", q=P)
                                for (at, m, hi), (_, _, lo) in zip(pt_block(0, q, j0, n), pt_block(1, q, j0, n)):
                                    ins = nc.vector.tensor_tensor(lo, src[:, at:at + m, :], f32(hi), ALU.subtract)
                                ins.then_inc(s_tlo, 1)
                        elif op[0] == "X":
                            x1_lo(tile_of(op), tp[tile_of(op) % 2][:, :], tile_of(op) + 1)
                        elif op == "M":
                            dve.wait_ge(s_mean, 1)
                            for dst, k in ((scales, 1.0), (above, 0.5), (below, -0.5)):
                                nc.vector.tensor_scalar(dst, accum[0][:, 0:3], k / (HIDDEN * D), None, ALU.mult
                                                        ).then_inc(s_thr, 1)
                            dve.wait_ge(s_thr, 3)
                            nc.vector.tensor_tensor(squared, scales[:, 2:3], scales[:, 2:3], ALU.mult).then_inc(s_thr, 1)
                    if h.turn is None and h.n >= TERNARY:
                        for n in ternary_in_head(h.n, i, 1):
                            ternary(n)
                    if h.n >= NH - 1:
                        k = (h.n - (NH - 1)) * QT + i
                        if k in DVE_SECOND:
                            second_stats(-1, DVE_SECOND[k])
                        if k in DVE_FIRST:
                            first_stats(-1, DVE_FIRST[k])
                if "O" in h.steps[QT - 1]:
                    add_out(h, QT - 1)
                if h.n == 0:
                    dve.wait_ge(s_abs, PIECES)
                    nc.vector.tensor_reduce(totals, abssum.rearrange("p (w m) -> p w m", w=3), AX.X, ALU.add
                                            ).then_inc(s_tot, 1)
                    dve.wait_ge(s_acczero, 1)
                    dve.wait_ge(s_const, 4)

            def group(g, first, more):
                at = lambda per, off: g * per + off
                for m in range(MC):
                    dve.wait_ge(s_silu, at(MC, m + 1))
                    if m or not first:
                        dve.wait_ge(s_glo, at(MC, m))
                    nc.vector.scalar_tensor_tensor(ghid, score[m % 2][:, HALF:2 * HALF], scales[:, 1:2], gate,
                                                   ALU.mult, ALU.mult).then_inc(s_gated, 1)
                    if first:
                        for n in ternary_in_group(m, 1):
                            ternary(n)
                    if more and m in CHUNK_SECOND and m < MC - 1:
                        second_stats(g, CHUNK_SECOND[m])
                    if more and m in CHUNK_FIRST:
                        first_stats(g, CHUNK_FIRST[m])
                    dve.wait_ge(s_ghi, at(MC, m + 1))
                    nc.vector.tensor_tensor(gt[1][m], ghid, f32(gt[0][m]), ALU.subtract).then_inc(s_glo, 1)
                if more:
                    second_stats(g, CHUNK_SECOND[MC - 1])
                for j in range(GT):
                    if more and j < 2:
                        for k in (2 * j, 2 * j + 1):
                            x1_lo(k, x1_bank(k), at(GT, GT + k + 1))
                    dve.wait_ge(s_f, at(GT, j + 1))
                    nc.vector.bn_stats(stats3[:, j, :], ff_bank(j)).then_inc(s_obn, 1)
                    dve.wait_ge(s_obn, at(GT, j + 1))
                    alone(dve, 1)
                    nc.vector.bn_aggr(mv3[:, j, :], stats3[:, j, :]).then_inc(s_ovar, 1)

            group(0, True, True)
            with dve.Fori(1, G - 1) as g:
                group(g, False, True)
            group(G - 1, False, False)

        @block.tensor
        def _(pe):
            pe.wait_ge(s_const, 4)

            def x_transpose(n, free):
                pe.wait_ge(s_xn, n + 1)
                if free:
                    pe.wait_ge(*free)
                for c in range(C):
                    ins = nc.tensor.transpose(tp[n % 2][:, c * P:(c + 1) * P], xin[:, n % 4, c * P:(c + 1) * P],
                                              identity[:, :])
                ins.then_inc(s_xt, 1)

            def project(op, batch, bank):
                first = int(op[1]) * HALF
                w = {"K": w_k, "V": w_v, "Q": w_q}[op[0]]
                for c in range(C):
                    for k, (a, b) in enumerate(((0, 0), (0, 1), (1, 0))):
                        ins = nc.tensor.matmul(accum[bank][:, :], w[:, a, c, :],
                                               xnt_flat[:, x_columns(batch, b, c, first, HALF)],
                                               start=(c == 0 and k == 0), stop=(c == C - 1 and k == 2))
                ins.then_inc(s_proj, 1)

            def v_transpose(op, bank):
                base = 4 * (op == "VB")
                for j in range(4):
                    ins = nc.tensor.transpose(tp[bank][:, j * P:(j + 1) * P], vt[:, (base + j) * P:(base + j + 1) * P],
                                              identity[:, :])
                ins.then_inc(s_vt, 1)

            for n in range(8):
                x_transpose(n, (s_xlo, n - 1) if n >= 2 else None)
            pe.wait_ge(s_xlo, 8)
            for n, op in enumerate(("K0", "K1", "V0", "V1")):
                pe.wait_ge(s_split[op[0].lower()], 1)
                if n >= 2:
                    pe.wait_ge(s_projlo, n - 1)
                project(op, 0, n % 2)
            for n in range(8, 12):
                x_transpose(n, (s_xlo, n - 1))
            for n, op in enumerate(("VA", "VB")):
                pe.wait_ge(s_projlo, 4)
                pe.wait_ge(s_xlo, 11 + n)
                v_transpose(op, n)
            for n, op in enumerate(("Q0", "Q1")):
                pe.wait_ge(s_split["q"], 1)
                pe.wait_ge(s_projlo, 3 + n)
                project(op, 0, n)
            for n in range(12, XT):
                x_transpose(n, (s_vlo, n - 11) if n < 14 else (s_xlo, n - 1))

            def acc_free(h, op):
                was = h.before[op]
                back = was.endswith("-")
                was = was.rstrip("-")
                if was == "M":
                    pe.wait_ge(s_thr, 3)
                elif was in PROJ:
                    pe.wait_ge(s_projlo, h.at(6, PROJ[was] + (0 if back else 6)))
                elif was == "PV0":
                    pe.wait_ge(s_zlo, h.at(2, 1 - 2 * back))
                elif was == "PV1":
                    pe.wait_ge(s_zlo, h.at(2, 0))
                else:
                    pe.wait_ge(s_sum, h.at(QT, tile_of(was) + 1 - QT * back))

            def tp_free(h, op, bank):
                if h.n == 0 and op in ("T0", "T1"):
                    pe.wait_ge(s_xlo, XT)
                    return
                was, _ = TP_BEFORE[op, bank]
                if was == "VB" and h.steps is LAST:
                    was = "T1"
                if was[0] == "V":
                    pe.wait_ge(s_vlo, h.at(2, 3 + (was == "VB")))
                    return
                q = int(was[1])
                previous = q == 7 or was.endswith("-")
                pe.wait_ge(s_tlo, h.at(FILLS, FILL[q] + 1 + (bank == 1 and q >= 4) - FILLS * previous))

            def scores(h, i):
                if i == 0:
                    pe.wait_ge(s_projlo, h.at(6, PROJ["Q0"]))
                if i == 4:
                    pe.wait_ge(s_projlo, h.at(6, PROJ["Q1"]))
                if i >= 2 or h.n > 0:
                    pe.wait_ge(s_exp, h.at(QT, i - 1))
                dst, slot = score[i % 2], h.slot(0)
                q = slice(i * P, (i + 1) * P)
                banks = [(0, WIDTH[i])] if i < 4 else [(0, HALF), (HALF, HALF + WIDTH[i - 4])]
                for b, (k0, k1) in enumerate(banks):
                    for n, (a, c) in enumerate(((0, 0), (0, 1), (1, 0))):
                        nc.tensor.matmul(dst[:, k0:k1], qt[:, a, q], kt[:, slot, c, k0:k1],
                                         start=(n == 0), stop=(n == 2 and b < i // 4))
                nc.tensor.matmul(dst[:, i * P:(i + 1) * P], identity_b[:, :], mask[:, :], start=False, stop=True
                                 ).then_inc(s_score, 1)

            def p_transpose(h, op):
                q = tile_of(op)
                pe.wait_ge(s_norm, h.at(QT, q + 1 - (QT if q == 7 else 0)))
                for bank, j0, n in fills_of(op):
                    tp_free(h, op, bank)
                    for j in range(n):
                        ins = nc.tensor.transpose(tp[bank][:, j * P:(j + 1) * P],
                                                  probs[:, q % 2, (j0 + j) * P:(j0 + j + 1) * P], identity[:, :])
                    ins.then_inc(s_t, 1)

            def values(h, op):
                group = int(op[2])
                slot = h.slot(-1 if group else 0)
                back = FILLS if group else 0
                pe.wait_ge(s_tlo, h.at(FILLS, (FILL[7] + 2 if group else FILL[3] + 1) - back))
                if not group:
                    pe.wait_ge(s_vlo, h.at(2, 2))
                dst = accum[ACC_BANK[op]]
                tiles = 4 * group + 4
                for j in range(tiles):
                    first = max(0, j - 4 * group)
                    q = slice(min(first, 2) * P, HALF)
                    for n, (a, b) in enumerate(((0, 0), (0, 1), (1, 0))):
                        ins = nc.tensor.matmul(dst[:, q], v[:, slot, a, j * P:(j + 1) * P],
                                               pt[:, b, key_slot(group, j), q],
                                               start=(j == 0 and n == 0), stop=(j == tiles - 1 and n == 2))
                ins.then_inc(s_pv, 1)

            def output(h, i):
                slot = h.slot(-1)
                if i == 0:
                    pe.wait_ge(s_split["o"], h.at(1, 0))
                    pe.wait_ge(s_zlo, h.at(2, -1))
                if i == 4:
                    pe.wait_ge(s_zlo, h.at(2, 0))
                for n, (a, b) in enumerate(((0, 0), (0, 1), (1, 0))):
                    ins = nc.tensor.matmul(accum[ACC_BANK[f"O{i}"]][:, :], zt[:, a, i * P:(i + 1) * P],
                                           w_o[:, slot, b, :], start=(n == 0), stop=(n == 2))
                ins.then_inc(s_o, 1)

            def x1_transpose(j, count, bank, free):
                pe.wait_ge(s_x1n, count)
                pe.wait_ge(*free)
                for c in range(C):
                    ins = nc.tensor.transpose(bank[:, c * P:(c + 1) * P], x1n[:, j, c * P:(c + 1) * P], identity[:, :])
                ins.then_inc(s_x1t, 1)

            pe.wait_ge(s_ptzero, 1)
            for h in heads_of(pe):
                if h.n < NH - 1 or h.turn is not None:
                    batch = h.at(1, 1) // HEADS
                    if h.turn is not None:
                        batch = pe.snap(batch)
                for i, step in enumerate(h.steps):
                    for op in step:
                        if op == "S":
                            scores(h, i)
                        elif op in PROJ:
                            pe.wait_ge(s_split[op[0].lower()], h.at(1, 2))
                            acc_free(h, op)
                            project(op, batch, ACC_BANK[op])
                        elif op in ("VA", "VB"):
                            pe.wait_ge(s_projlo, h.at(6, 6 + PROJ["V1" if op == "VB" else "V0"]))
                            tp_free(h, op, 1)
                            v_transpose(op, 1)
                        elif op in ("PV0", "PV1"):
                            acc_free(h, op)
                            values(h, op)
                        elif op == "O":
                            acc_free(h, f"O{i}")
                            output(h, i)
                        elif op == "M":
                            acc_free(h, op)
                            pe.wait_ge(s_tot, 1)
                            nc.tensor.matmul(accum[0][:, 0:3], ones[:, :], totals, start=True, stop=True
                                             ).then_inc(s_mean, 1)
                        elif op[0] == "X":
                            j = tile_of(op)
                            free = (s_tlo, h.at(FILLS, FILL[7] + 1 + j - FILLS)) if j < 2 else (s_x1lo, j - 1)
                            x1_transpose(j, j + 1, tp[j % 2][:, :], free)
                        else:
                            p_transpose(h, op)

            def group(g, first, more):
                at = lambda per, off: g * per + off
                for m in range(MC):
                    if first:
                        pe.wait_ge(s_tern, 2 * m + 2)
                    if m < 2:
                        pe.wait_ge(s_x1lo, at(GT, 4))
                    else:
                        pe.wait_ge(s_gated, at(MC, m - 1))
                    for w in range(2):
                        for c in range(C):
                            for b in range(2):
                                ins = nc.tensor.matmul(score[m % 2][:, w * HALF:(w + 1) * HALF], w13t[:, m, w, c, :],
                                                       x1nt[:, b, c, :], start=(c == 0 and b == 0),
                                                       stop=(c == C - 1 and b == 1))
                    ins.then_inc(s_h, 1)
                for j in range(GT):
                    if not first:
                        pe.wait_ge(s_onorm, at(GT, j + 1 - GT))
                    elif j == 0:
                        pe.wait_ge(s_sum, QT + QT * NH)
                    for m in range(MC):
                        if j == 0:
                            pe.wait_ge(s_glo, at(MC, m + 1))
                            if first:
                                pe.wait_ge(s_tern, 2 * MC + m + 1)
                        for a in range(2):
                            ins = nc.tensor.matmul(ff_bank(j), gt[a][m][:, j * P:(j + 1) * P], w2t[:, m, :],
                                                   start=(m == 0 and a == 0), stop=(m == MC - 1 and a == 1))
                    ins.then_inc(s_f, 1)
                    if more and j < 2:
                        for k in (2 * j, 2 * j + 1):
                            x1_transpose(k, at(GT, GT + k + 1), x1_bank(k), (s_gated, at(MC, MC - 1 + j)))

            group(0, True, True)
            with pe.Fori(1, G - 1) as g:
                group(g, False, True)
            group(G - 1, False, False)


def kernel(**inputs):
    import numpy as np
    import concourse.bacc as bacc
    from concourse.bass_utils import run_bass_kernel_spmd

    a = {k: np.asarray(val) for k, val in inputs.items()}

    def by_model_dim(w):
        return np.ascontiguousarray(w.reshape(HEADS, E, C, P).transpose(0, 3, 2, 1)).reshape(HEADS, P, C * E)

    def ffn_in(w):
        w = np.pad(w, ((0, MC * P - HIDDEN), (0, 0))).reshape(MC, P, C, P)
        return np.ascontiguousarray(w.transpose(3, 0, 2, 1)).reshape(P, MC, C * P)

    w2 = np.pad(a["L0_ffn_w2"].T, ((0, MC * P - HIDDEN), (0, 0))).reshape(MC, P, D)
    arrays = {
        "x": np.ascontiguousarray(a["L0_attn_x"].reshape(TOK, D)),
        "wq": by_model_dim(a["L0_attn_W_Q"]),
        "wk": by_model_dim(a["L0_attn_W_K"]),
        "wv": by_model_dim(a["L0_attn_W_V"]),
        "wo": np.ascontiguousarray(a["L0_attn_W_O"].transpose(0, 2, 1)),
        "w1": ffn_in(a["L0_ffn_w1"]),
        "w3": ffn_in(a["L0_ffn_w3"]),
        "w2": np.ascontiguousarray(w2.transpose(1, 0, 2)),
    }
    nc = bacc.Bacc("TRN2", target_bir_lowering=False, num_devices=1, dynamic_dma_scratch_size=4096)
    args = [nc.dram_tensor(name, val.shape, mybir.dt.from_np(val.dtype), kind="ExternalInput").ap()
            for name, val in arrays.items()]
    out = nc.dram_tensor("out", [TOK, D], F32, kind="ExternalOutput").ap()
    block_kernel(nc, *args, out)
    r = run_bass_kernel_spmd(nc, [arrays], core_ids=[0])
    return r.results[0]["out"].reshape(BATCH, SEQ, D)
```

```python
from contextlib import ExitStack

import concourse.bass as bass
from concourse import mybir

ALU = mybir.AluOpType
ACT = mybir.ActivationFunctionType
AX = mybir.AxisListType
F32 = mybir.dt.float32
F32R = mybir.dt.float32r
BF16 = mybir.dt.bfloat16

P = 128
BATCH, SEQ, D = 2, 1024, 512
HEADS, E = 16, 128
HIDDEN = int(2 * D * 4 / 3)
C = D // P
QT = SEQ // P
TOK = BATCH * SEQ
XT = TOK // P
NH = BATCH * HEADS
BODY = 4
TURNS = (NH - BODY) // BODY
MEET = HEADS // BODY - 1
HALF = 512
MC = -(-HIDDEN // P)
G = TOK // HALF
GT = HALF // P
QUADS = NH // BODY
SCALE = float(E) ** -0.5
MASKED = -1.0e9 / SCALE
EPS = 1e-5

WIDTH = [256, 256, 384, 512]
FILL = [0, 1, 2, 3, 4, 6, 8, 10]
FILLS = 12

FULL = [["S", "K0", "T7", "O"], ["S", "K1", "PV1", "T0", "O"], ["S", "T1", "V0", "O"], ["S", "T2", "V1", "T3", "O"],
        ["S", "O"], ["S", "PV0", "T4", "O"], ["S", "Q0", "T5", "O"], ["S", "Q1", "T6", "O"]]
FIRST = [[op for op in s if op not in ("T7", "PV1", "O")] for s in FULL]
MEANS = [FULL[0] + ["M"]] + FULL[1:]
LAST = [["S", "T7", "O"], ["S", "PV1", "T0", "O"], ["S", "T1", "O"], ["S", "T2", "O"], ["S", "T3", "O"],
        ["S", "PV0", "T4", "O"], ["S", "T5", "O"], ["S", "T6", "O"]]
TAIL = [["T7", "O"], ["O"], ["PV1", "O"], ["X0", "O"], ["X1", "O"], ["X2", "O"], ["X3", "O"], ["O"]]
PROJ = {"K0": 1, "K1": 2, "V0": 3, "V1": 4, "Q0": 5, "Q1": 6}

ACC_BANK = {"K0": 0, "O0": 1, "K1": 0, "PV1": 1, "O1": 0, "V0": 1, "O2": 0, "V1": 1, "O3": 0, "O4": 1,
            "PV0": 0, "O5": 1, "Q0": 0, "O6": 1, "Q1": 0, "O7": 1}
ACC_BEFORE = {"K0": "Q1-", "O0": "O7-", "K1": "K0", "PV1": "O0", "O1": "K1", "V0": "PV1", "O2": "O1", "V1": "V0",
              "O3": "O2", "O4": "V1", "PV0": "O3", "O5": "O4", "Q0": "PV0", "O6": "O5", "Q1": "Q0", "O7": "O6"}
ACC_BEFORE_FIRST = {"K0": "Q1-", "K1": "K0", "V0": "Q1-", "V1": "V0", "PV0": "K1", "Q0": "PV0", "Q1": "Q0"}
ACC_BEFORE_MEANS = {**ACC_BEFORE, "M": "K0", "K1": "M"}
ACC_BEFORE_LAST = {**ACC_BEFORE, "O1": "Q1-", "O4": "PV1"}
ACC_BEFORE_TAIL = {"O0": "O7-", "O1": "PV0-", "PV1": "O0", "O2": "O1", "O3": "O2", "O4": "PV1", "O5": "O4",
                   "O6": "O5", "O7": "O6"}
TP_BEFORE = {("T7", 0): ("T6-", 0), ("T7", 1): ("T6-", 1), ("T0", 0): ("T7", 0), ("T1", 1): ("T7", 1),
             ("T2", 0): ("T0", 0), ("T3", 0): ("T2", 0), ("T4", 0): ("T3", 0), ("T4", 1): ("T1", 1),
             ("T5", 0): ("T4", 0), ("T5", 1): ("T4", 1), ("T6", 0): ("T5", 0), ("T6", 1): ("T5", 1)}
PIECES = 3 * MC
TERNARY = NH - 3
LATE = 3 * QT - 1
FIRST_STATS, FIRST_APPLY, SECOND_STATS, SECOND_APPLY = ({2 * j + k: j for j in range(GT)} for k in range(4))
CHUNK_FIRST, CHUNK_SECOND = ({2 * j + k: j for j in range(GT)} for k in (1, 3))
NX = 8
WEIGH = 8
ONE_BANK = {"T0": 0, "T1": 1, "T2": 0, "T3": 0}


class Head:

    def __init__(self, n, turn=None, steps=FULL, before=ACC_BEFORE, next_batch=None):
        self.n, self.turn, self.steps, self.before = n, turn, steps, before
        self.next_batch = (n + 1) // HEADS if turn is None else next_batch

    def at(self, per_head, offset):
        fixed = per_head * self.n + offset
        return fixed if self.turn is None else self.turn * (BODY * per_head) + fixed

    def slot(self, n):
        return (self.n + n) % 2


def heads_of(eng):
    yield Head(0, steps=FIRST, before=ACC_BEFORE_FIRST)
    with eng.Fori(0, MEET) as turn:
        for k in range(BODY):
            yield Head(1 + k, turn, next_batch=0)
    for k in range(BODY):
        yield Head(BODY * MEET + 1 + k)
    with eng.Fori(MEET + 1, TURNS) as turn:
        for k in range(BODY):
            yield Head(1 + k, turn, next_batch=1)
    yield Head(NH - 3, steps=MEANS, before=ACC_BEFORE_MEANS)
    yield Head(NH - 2)
    yield Head(NH - 1, steps=LAST, before=ACC_BEFORE_LAST)
    yield Head(NH, steps=TAIL, before=ACC_BEFORE_TAIL)


def block_kernel(nc, x, wq, wk, wv, wo, w1, w3, w2, out):
    ctx = ExitStack()
    with ctx:
        def sem(name):
            return ctx.enter_context(nc.semaphore(name))

        R_COLS = 2 * C * TOK + 6 * 2 * C * E + 2 * 2 * SEQ + 2 * SEQ + 5 * SEQ + 2 * SEQ + 2 * QT * HALF
        F_COLS = 4 * 512 + 2 * SEQ + QT * D
        with nc.sbuf_tensor("arena_late", [P, R_COLS], F32) as arena_late:
            pass
        arena_r = ctx.enter_context(nc.sbuf_tensor("arena_r", [P, R_COLS], F32R))
        arena_f = ctx.enter_context(nc.sbuf_tensor("arena_f", [P, F_COLS], F32))
        taken = {"r": 0, "f": 0}
        start = {}

        def f32(ap):
            return ap.bitcast(F32)

        def at_column(which, first, *shape):
            n = 1
            for s in shape:
                n *= s
            assert first + n <= (F_COLS if which == "f" else R_COLS)
            a = {"r": arena_r, "late": arena_late, "f": arena_f}[which][:, first:first + n]
            names = "abcd"[:len(shape)]
            sizes = {names[i]: shape[i] for i in range(1, len(shape))}
            return a.rearrange(f"p ({' '.join(names)}) -> p {' '.join(names)}", **sizes)

        def take(which, name, *shape):
            start[name] = taken[which]
            a = at_column(which, start[name], *shape)
            n = 1
            for s in shape:
                n *= s
            taken[which] += n
            return a

        xnt = take("r", "xnt", BATCH, 2, C * SEQ)
        w_k = take("r", "w_k", 2, C, E)
        w_v = take("r", "w_v", 2, C, 2 * E)
        w_q = take("r", "w_q", 2, C, E)
        w_o = take("r", "w_o", 2, 2, C * E)
        kt = take("r", "kt", 2, 2, SEQ)
        qt = take("r", "qt", 2, SEQ)
        v_low = take("r", "v_low", 3, 2, QT // 2 * E)
        v_high = take("r", "v_high", 2, 2, QT // 2 * E)
        zt = take("r", "zt", 2, SEQ)
        pt = take("r", "pt", 2, QT, HALF)
        raw_k, raw_v, raw_q, raw_o = (take("f", f"raw_{w}", D) for w in "kvqo")
        probs = take("f", "probs", 2, SEQ)
        acc = take("f", "acc", QT, D)
        xnt_flat = xnt.rearrange("p a b s -> p (a b s)")
        xnt_by_chunk = xnt.rearrange("p a b (c s) -> p a b c s", c=C)
        weigh = acc

        w13t = at_column("r", 0, MC, 2, C, P)
        w2t = at_column("r", MC * 2 * D, MC, D)
        w2t_end = MC * 3 * D
        assert w2t_end <= start["w_v"]
        extra = ctx.enter_context(nc.sbuf_tensor("extra", [P, 6 * D], F32)).rearrange("p (a b) -> p a b", b=D)
        xin = [at_column("f", start["probs"] + k * D, D) for k in range(4)] + [extra[:, k, :] for k in range(4)]
        is_less = [extra[:, 0, :], extra[:, 1, :], raw_q]
        wraw = [extra[:, 2, :], extra[:, 3, :], raw_k]
        stage = [extra[:, 4:6, :], at_column("late", start["w_v"], 2, D)]
        x1_next = at_column("late", start["kt"], GT, D)
        x1n = at_column("late", start["v_low"], GT, D)
        x1nt = at_column("r", start["pt"], 2, C, HALF)
        spare = [first + k * HALF for first, last in ((start["kt"] + 2 * SEQ, start["v_low"]),
                                                      (start["v_low"] + 2 * SEQ, start["pt"]),
                                                      (start["pt"] + 2 * C * HALF, R_COLS))
                 for k in range((last - first) // HALF)]
        gt = [[at_column("r", spare[2 * m + a], HALF) for m in range(MC)] for a in range(2)]
        x1_now = at_column("f", start["probs"], GT, D)
        fin = at_column("f", start["acc"], GT, D)
        gate = raw_o
        ghid = raw_v

        small = ctx.enter_context(nc.sbuf_tensor("small", [P, 256], F32))
        negmax, rowsum, rinv = small[:, 0:8], small[:, 8:16], small[:, 16:24]
        stats = small[:, 24:36].rearrange("p (a b) -> p a b", b=6)
        mv = small[:, 36:40].rearrange("p (a b) -> p a b", b=2)
        varp = small[:, 40:42]
        rstd = small[:, 42:44]
        power = small[:, 44:45]
        shift = small[:, 45:47]
        totals = small[:, 48:51]
        scales = small[:, 51:54]
        above = small[:, 54:57]
        below = small[:, 57:60]
        squared = small[:, 71:72]
        abssum = small[:, 80:80 + PIECES]
        mv3 = small[:, 116:124].rearrange("p (a b) -> p a b", b=2)
        scaled3 = small[:, 124:128]
        rstd3 = small[:, 128:132]
        factor3 = small[:, 132:136]
        shift3 = small[:, 136:140]
        stats3 = small[:, 150:174].rearrange("p (a b) -> p a b", b=6)
        stats_x = small[:, 174:174 + 6 * NX].rearrange("p (a b) -> p a b", b=6)
        mv_x = small[:, 222:222 + 2 * NX].rearrange("p (a b) -> p a b", b=2)
        varp_x, rstd_x = small[:, 238:238 + NX], small[:, 246:246 + NX]
        keep = small[:, 140:140 + TURNS]
        identity = ctx.enter_context(nc.sbuf_tensor("identity", [P, P], F32))
        ones = ctx.enter_context(nc.sbuf_tensor("ones", [P, P], F32))
        identity_b = ctx.enter_context(nc.sbuf_tensor("identity_b", [P, P], BF16))
        mask = ctx.enter_context(nc.sbuf_tensor("mask", [P, P], BF16))

        score = [ctx.enter_context(nc.psum_tensor(f"score{i}", [P, SEQ], F32)) for i in range(2)]
        tp = [ctx.enter_context(nc.psum_tensor(f"tp{i}", [P, HALF], F32)) for i in range(2)]
        accum = [ctx.enter_context(nc.psum_tensor(f"accum{i}", [P, HALF], F32)) for i in range(2)]

        running = nc.dram_tensor("running", [BATCH, P, QT, D], F32, kind="Internal").ap()

        s_const = sem("s_const")
        s_mask = sem("s_mask")
        s_xin = [sem(f"s_xin{i}") for i in range(NX)]
        s_bn, s_var = sem("s_bn"), sem("s_var")
        s_eps, s_rstd = sem("s_eps"), sem("s_rstd")
        s_centred = sem("s_centred")
        s_xn = [sem("s_xn_even"), sem("s_xn_odd")]
        s_xt, s_xhi, s_xlo = sem("s_xt"), sem("s_xhi"), sem("s_xlo")
        s_raw = {w: sem(f"s_raw_{w}") for w in "kvqo"}
        s_split_hi = {w: sem(f"s_split_hi_{w}") for w in "kvqo"}
        s_split = {w: sem(f"s_split_{w}") for w in "kvqo"}
        s_proj, s_projhi, s_projlo = sem("s_proj"), sem("s_projhi"), sem("s_projlo")
        s_score, s_negmax, s_exp = sem("s_score"), sem("s_negmax"), sem("s_exp")
        s_rinv, s_norm = sem("s_rinv"), sem("s_norm")
        s_t, s_thi, s_tlo = sem("s_t"), sem("s_thi"), sem("s_tlo")
        s_pv, s_zhi, s_zlo = sem("s_pv"), sem("s_zhi"), sem("s_zlo")
        s_o = sem("s_o")
        s_sum = sem("s_sum")
        s_part = sem("s_part")
        s_accfree = sem("s_accfree")
        s_passed = [sem("s_passed_pool"), sem("s_passed_dve")]
        s_ptzero = sem("s_ptzero")
        s_weigh = [sem(f"s_weigh{i}") for i in range(WEIGH)]
        s_acczero = sem("s_acczero")
        s_w = [sem(f"s_w{i}") for i in range(3)]
        s_abs = sem("s_abs")
        s_tot, s_mean, s_thr = sem("s_tot"), sem("s_mean"), sem("s_thr")
        s_less, s_tern = sem("s_less"), sem("s_tern")
        s_stage = [sem(f"s_stage{i}") for i in range(2)]
        s_fbn, s_fvar, s_feps, s_frstd = sem("s_fbn"), sem("s_fvar"), sem("s_feps"), sem("s_frstd")
        s_shift = sem("s_shift")
        s_y, s_x1 = sem("s_y"), sem("s_x1")
        s_x1n, s_x1t = sem("s_x1n"), sem("s_x1t")
        s_x1hi, s_x1lo = sem("s_x1hi"), sem("s_x1lo")
        s_now = sem("s_now")
        s_h, s_silu, s_gated, s_ghi, s_glo = (sem(f"s_{n}") for n in ("h", "silu", "gated", "ghi", "glo"))
        s_f = sem("s_f")
        s_obn, s_ovar, s_oeps, s_orstd = sem("s_obn"), sem("s_ovar"), sem("s_oeps"), sem("s_orstd")
        s_oscale = sem("s_oscale")
        s_oshift, s_onorm, s_fin, s_out = sem("s_oshift"), sem("s_onorm"), sem("s_fin"), sem("s_out")

        block = ctx.enter_context(nc.Block())

        def fill(h, i, second=False):
            return h.at(FILLS, FILL[i] + 1 + second)

        def key_slot(group, j):
            return QT - 1 if j == 4 * group + 3 else j

        def alone(eng, which):
            eng.sem_inc(s_passed[which], 1)

        def tile_of(op):
            return int(op[1:])

        def fills_of(op):
            if op in ONE_BANK:
                return [(ONE_BANK[op], 0, tile_of(op) + 1)]
            return [(0, 0, 4), (1, 4, tile_of(op) - 3)]

        def pt_block(hilo, i, j0, n):
            q = slice(i % 4 * P, (i % 4 + 1) * P)
            js = list(range(j0, j0 + n))
            last = 4 * (i // 4) + 3
            runs = []
            if last in js and key_slot(i // 4, last) != last:
                js.remove(last)
                runs = [(last - j0, 1, pt[:, hilo, QT - 1:QT, q])]
            return [(js[0] - j0, len(js), pt[:, hilo, js[0]:js[0] + len(js), q])] + runs

        def x_columns(batch, hilo, c, first, n):
            return bass.ds(batch * (2 * C * SEQ) + ((hilo * C + c) * SEQ + first), n)

        def splits_at(h, i):
            left = NH - 1 - h.n if h.turn is None else NH
            if i == 0 and left >= 1:
                yield "q", h.at(1, 2), h.at(16, 32), h.at(6, 6)
            if i == 2 and left >= 2:
                yield "k", h.at(1, 3), h.at(16, 48), h.at(6, 8)
            if h.n % 2 == 0 and i in (4, 6) and left >= i // 2:
                yield ("v", i // 2 % 2), h.at(1, 1 + i // 2), h.at(16, 16 + 8 * i), h.at(6, 10)
            if i == 6 and left >= 0:
                yield ("o", h.slot(0)), h.at(1, 1), h.at(16, 16), None

        def v_slot(h, back):
            n = h.n - back
            return 1 + n // 2 % 2 if n % 2 else 0

        def v_places(h, op, hilo):
            cols = slice(int(op[1]) * 2 * E, (int(op[1]) + 1) * 2 * E)
            if h.n % 2:
                odd = v_slot(h, -2)
                a = v_low[:, 0:odd + 1:odd, hilo, cols]
            else:
                a = v_high[:, 0:2, hilo, cols]
            return a.rearrange("p h (t e) -> p h t e", e=E)

        def v_bank(bank):
            return accum[bank][:, :].rearrange("p (t h e) -> p h t e", t=2, h=2)

        def weight_parts(w):
            raw = {"k": raw_k, "v": raw_v, "q": raw_q, "o": raw_o}[w[0]]
            if w[0] == "o":
                return raw, w_o[:, w[1], 0, :], w_o[:, w[1], 1, :]
            if w[0] == "v":
                dims = slice(w[1] * E, (w[1] + 1) * E)
                return raw.rearrange("p (c e) -> p c e", c=C), w_v[:, 0, :, dims], w_v[:, 1, :, dims]
            dst = {"k": w_k, "q": w_q}[w]
            return [raw] + [dst[:, p, :, :].rearrange("p c e -> p (c e)") for p in range(2)]

        def ternary_place(n):
            if n < 2 * MC:
                return w13t[:, n // 2, n % 2, :, :].rearrange("p c h -> p (c h)")
            return w2t[:, n - 2 * MC, :]

        def weight_of(n):
            return (n % 2, n // 2) if n < 2 * MC else (2, n - 2 * MC)

        def ternary_in_head(n, i, lag):
            k = (n - TERNARY) * QT + i - 1 - lag
            return [k] if 0 <= k < LATE else []

        def ternary_in_group(m, lag):
            k = LATE + m - lag
            return [k] if LATE <= k < PIECES else []

        def piece_slot(n):
            return n % 2 if n < LATE else (n - LATE) % 3

        def slot_use(n):
            uses = [k for k in range(n + 1) if piece_slot(k) == piece_slot(n)]
            return len(uses), uses[-2] if len(uses) > 1 else None

        def x1_bank(j):
            return score[(j // 2 + 1) % 2][:, j % 2 * HALF:(j % 2 + 1) * HALF]

        def ff_bank(j):
            return (tp + accum)[j][:, :]

        def x_bank(n):
            return [tp[0][:, :], tp[1][:, :], score[1][:, 0:HALF], score[1][:, HALF:SEQ]][n % 4]

        @block.sync
        def _(sp):
            def load(w, src, head):
                dst = {"k": raw_k, "v": raw_v, "q": raw_q, "o": raw_o}[w]
                sp.dma_start(dst, src[head]).then_inc(s_raw[w], 16)

            def load_weight(n):
                which, m = weight_of(n)
                slot, before = piece_slot(n), slot_use(n)[1]
                if before is not None:
                    sp.wait_ge(s_tern, before + 1)
                elif slot >= 2:
                    sp.wait_ge(s_split["k"], NH)
                sp.dma_start(wraw[slot], (w1, w3, w2)[which][:, m, :]).then_inc(s_w[slot], 16)

            def loads_at(n, i):
                k = (n - TERNARY) * QT + i
                at = (0, 1) if k == 0 else () if k == 1 else (k - 1, k) if i == 0 else (k,)
                return [p for p in at if p < LATE]

            def load_tile(g, j):
                if j >= 2 or not (isinstance(g, int) and g < 0):
                    sp.wait_ge(s_x1, g * GT + (GT + j - 1))
                b, half = (g + 1) // 2, (g + 1) % 2
                sp.dma_start(stage[j % 2][:, 0:1, :], running[bass.ds(b, 1), :, bass.ds(half * 4 + j, 1), :]
                             .rearrange("q p a d -> p q (a d)")).then_inc(s_stage[j % 2], 16)
                sp.dma_start(stage[j % 2][:, 1, :], x[bass.ds(g * HALF + (HALF + j * P), P), :]
                             ).then_inc(s_stage[j % 2], 16)

            def load_x(n):
                if n >= NX:
                    sp.wait_ge(s_xt, n - NX + 1)
                sp.dma_start(xin[n % NX], x[n * P:(n + 1) * P, :]).then_inc(s_xin[n % NX], 16)

            for n in range(4):
                load_x(n)
            load("k", wk, 0)
            load("v", wv, 0)
            load("q", wq, 0)
            load("o", wo, 0)
            for n in range(4, 12):
                load_x(n)
            sp.wait_ge(s_split["k"], 1)
            load("k", wk, 1)
            sp.wait_ge(s_split["v"], 1)
            load("v", wv, 1)
            load_x(12)
            load_x(13)
            sp.wait_ge(s_split["q"], 1)
            load("q", wq, 1)
            load_x(14)
            load_x(15)
            sp.wait_ge(s_split["k"], 2)
            load("k", wk, 2)
            sp.wait_ge(s_split["v"], 2)
            load("v", wv, 2)
            sp.sem_inc(s_accfree, 1)
            for h in heads_of(sp):
                last = h.turn is None
                if not (last and h.n + 2 > NH - 1):
                    sp.wait_ge(s_split["q"], h.at(1, 2))
                    load("q", wq, h.at(1, 2) % HEADS)
                if not (last and h.n + 3 > NH - 1):
                    sp.wait_ge(s_split["k"], h.at(1, 3))
                    load("k", wk, h.at(1, 3) % HEADS)
                if h.n % 2 == 0 and not (last and h.n + 3 > NH - 1):
                    sp.wait_ge(s_split["v"], h.at(1, 3))
                    load("v", wv, h.at(1, 3) % HEADS)
                if h.n % BODY == 0 and not (last and h.n == 0):
                    quad = h.turn if h.turn is not None else h.n // BODY - 1
                    b = bass.ds(quad // (HEADS // BODY), 1)
                    sp.wait_ge(s_sum, h.at(QT, 4))
                    sp.dma_start(running[b, :, 0:4, :].rearrange("b p i d -> p (b i) d"), acc[:, 0:4, :]
                                 ).then_inc(s_part, 16)
                if last and TERNARY <= h.n < NH:
                    for i in range(QT if h.n == NH - 1 else QT - 1):
                        for n in loads_at(h.n, i):
                            load_weight(n)
                        if h.n == NH - 3 and i == 0:
                            load_tile(-1, 0)
                        if h.n == NH - 2 and i == 3:
                            sp.wait_ge(s_proj, 6 * (NH - 1) + PROJ["V1"])
                            load_tile(-1, 1)
                        if h.n == NH - 1 and i in (2, 4):
                            load_tile(-1, i // 2 + 1)
                        if h.n == NH - 1 and i == QT - 1:
                            for n in range(LATE, LATE + 3):
                                load_weight(n)
                if not (last and h.n + 1 > NH - 1):
                    sp.wait_ge(s_split["o"], h.at(1, 1))
                    load("o", wo, h.at(1, 1) % HEADS)
                if h.n % BODY == 0 and not (last and h.n == 0):
                    sp.wait_ge(s_sum, h.at(QT, 8))
                    sp.dma_start(running[b, :, 4:8, :].rearrange("b p i d -> p (b i) d"), acc[:, 4:8, :]
                                 ).then_inc(s_part, 16)
                    sp.wait_ge(s_part, quad * 32 + 32)
                    sp.sem_inc(s_accfree, 1)
                if h.n % 2 == 0 and not (last and h.n + 4 > NH - 1):
                    sp.wait_ge(s_split["v"], h.at(1, 4))
                    load("v", wv, h.at(1, 4) % HEADS)

            load_tile(0, 0)
            load_tile(0, 1)
            tiles = {LATE + 5: 2, LATE + 7: 3}
            for n in range(LATE + 3, PIECES):
                load_weight(n)
                if n in tiles:
                    load_tile(0, tiles[n])
            with sp.Fori(1, G - 1) as g:
                for j in range(GT):
                    load_tile(g, j)
            for j in range(GT):
                sp.wait_ge(s_fin, (G - 1) * GT + (j + 1))
                sp.dma_start(out[bass.ds((G - 1) * HALF + j * P, P), :], fin[:, j, :]).then_inc(s_out, 16)
            sp.wait_ge(s_out, 16 * G * GT)

        @block.gpsimd
        def _(pool):
            nc.gpsimd.memset(identity[:, :], 0.0).then_inc(s_mask, 1)
            nc.gpsimd.memset(mask[:, :], 0.0).then_inc(s_mask, 1)
            nc.gpsimd.memset(identity_b[:, :], 0.0).then_inc(s_mask, 1)
            nc.gpsimd.memset(power, -0.5).then_inc(s_mask, 1)
            for turn in range(TURNS):
                nc.gpsimd.memset(keep[:, turn:turn + 1], 0.0 if turn * BODY % HEADS == 0 else 1.0).then_inc(s_mask, 1)
            nc.gpsimd.memset(ones[:, :], 1.0).then_inc(s_const, 1)
            pool.wait_ge(s_mask, 4 + TURNS)
            for m in (identity, identity_b):
                nc.gpsimd.affine_select(out=m[:, :], in_=m[:, :], compare_op=ALU.not_equal, fill=1.0, base=0,
                                        pattern=[[-1, P]], channel_multiplier=1).then_inc(s_const, 1)
            nc.gpsimd.affine_select(out=mask[:, :], in_=mask[:, :], compare_op=ALU.is_ge, fill=MASKED, base=0,
                                    pattern=[[-1, P]], channel_multiplier=1).then_inc(s_const, 1)

            def rsqrt(n):
                pool.wait_ge(s_var, n + 2)
                k = slice(n % NX, n % NX + 2)
                nc.gpsimd.tensor_scalar(varp_x[:, k], mv_x[:, k, 1], EPS, None, ALU.add).then_inc(s_eps, 1)
                pool.wait_ge(s_eps, n // 2 + 1)
                nc.gpsimd.tensor_tensor(rstd_x[:, k], varp_x[:, k], power[:, 0:1].to_broadcast([P, 2]), ALU.pow
                                        ).then_inc(s_rstd, 1)

            def split(w, count):
                raw, hi, lo = weight_parts(w)
                pool.wait_ge(s_split_hi[w[0]], count)
                if not isinstance(count, int):
                    alone(pool, 0)
                nc.gpsimd.tensor_tensor(lo, raw, f32(hi), ALU.subtract).then_inc(s_split[w[0]], 1)

            def x_norm(n):
                pool.wait_ge(s_rstd, n // 2 + 1)
                k = n % NX
                nc.gpsimd.tensor_tensor(xin[k], xin[k], mv_x[:, k, 0:1].to_broadcast([P, D]), ALU.subtract
                                        ).then_inc(s_centred, 1)
                pool.wait_ge(s_centred, n // 2 + 1)
                nc.gpsimd.tensor_scalar(xin[k], xin[k], rstd_x[:, k:k + 1], 1.0, ALU.mult, ALU.mult
                                        ).then_inc(s_xn[1], 1)

            for n in range(XT):
                if n == 6:
                    split("k", 1)
                if n == 8:
                    split(("v", 0), 1)
                    split(("v", 1), 2)
                if n == 10:
                    split("q", 1)
                if n % 2:
                    x_norm(n)
                else:
                    rsqrt(n)
            split("k", 2)

            def less(n):
                if n == 0:
                    pool.wait_ge(s_thr, 4)
                slot, (use, before) = piece_slot(n), slot_use(n)
                pool.wait_ge(s_w[slot], 16 * use)
                if before is not None:
                    pool.wait_ge(s_tern, before + 1)
                elif slot >= 2:
                    pool.wait_ge(s_split["q"], NH)
                w = weight_of(n)[0]
                nc.gpsimd.tensor_scalar(is_less[slot], wraw[slot], below[:, w:w + 1], None, ALU.is_lt
                                        ).then_inc(s_less, 1)

            def tile_rsqrt(k, count):
                pool.wait_ge(s_fvar, count)
                alone(pool, 0)
                nc.gpsimd.tensor_scalar(varp[:, k:k + 1], mv[:, k, 1:2], EPS, None, ALU.add).then_inc(s_feps, 1)
                pool.wait_ge(s_feps, count)
                nc.gpsimd.tensor_tensor(rstd[:, k:k + 1], varp[:, k:k + 1], power, ALU.pow).then_inc(s_frstd, 1)
                pool.wait_ge(s_frstd, count)
                alone(pool, 0)
                nc.gpsimd.tensor_scalar(shift[:, k:k + 1], mv[:, k, 0:1], rstd[:, k:k + 1], -1.0, ALU.mult, ALU.mult
                                        ).then_inc(s_shift, 1)

            def first_step(g, j):
                at = lambda per, off: g * (per * GT) + (per * (GT + j) + off)
                pool.wait_ge(s_y, at(1, 1))
                if j == 0 and not (isinstance(g, int) and g < 0):
                    pool.wait_ge(s_now, g + 1)
                nc.gpsimd.tensor_tensor(x1_next[:, j, :], stage[j % 2][:, 0, :], stage[j % 2][:, 1, :], ALU.add
                                        ).then_inc(s_x1, 1)

            def first_factor(g, j):
                tile_rsqrt(0, g * (2 * GT) + (2 * (GT + j) + 1))

            def second_step(g, j):
                at = lambda per, off: g * (per * GT) + (per * (GT + j) + off)
                tile_rsqrt(1, at(2, 2))
            for h in heads_of(pool):
                if h.n == NH:
                    for i in range(QT, 2 * QT):
                        if i in SECOND_STATS:
                            second_step(-1, SECOND_STATS[i])
                    break
                fixed = h.turn is None
                for i in range(QT):
                    pool.wait_ge(s_rinv, h.at(QT, i + 1))
                    alone(pool, 0)
                    pr = probs[:, i % 2, 0:(i + 1) * P]
                    nc.gpsimd.tensor_scalar(pr, pr, rinv[:, i:i + 1], 1.0, ALU.mult, ALU.mult).then_inc(s_norm, 1)
                    for w, count, _, _ in splits_at(h, i):
                        split(w, count)
                    if fixed and h.n >= TERNARY:
                        for n in ternary_in_head(h.n, i, 0):
                            less(n)
                    if fixed and h.n == NH - 1:
                        if i in FIRST_APPLY:
                            first_step(-1, FIRST_APPLY[i])
                        if i in SECOND_STATS:
                            second_step(-1, SECOND_STATS[i])
                        if i in FIRST_STATS:
                            first_factor(-1, FIRST_STATS[i])
                if fixed and h.n == 0:
                    pool.wait_ge(s_abs, PIECES)
                    nc.gpsimd.memset(acc[:, :, :], 0.0).then_inc(s_acczero, 1)

            def finish(g):
                def scale_tile(j):
                    at = g * GT + (j + 1)
                    col = slice(j, j + 1)
                    pool.wait_ge(s_ovar, at)
                    alone(pool, 0)
                    nc.gpsimd.tensor_scalar(scaled3[:, col], mv3[:, j, 1:2], squared, EPS, ALU.mult, ALU.add
                                            ).then_inc(s_oeps, 1)
                    pool.wait_ge(s_oeps, at)
                    nc.gpsimd.tensor_tensor(rstd3[:, col], scaled3[:, col], power, ALU.pow).then_inc(s_orstd, 1)
                    pool.wait_ge(s_orstd, at)
                    nc.gpsimd.tensor_tensor(factor3[:, col], rstd3[:, col], scales[:, 2:3], ALU.mult
                                            ).then_inc(s_oscale, 1)
                    pool.wait_ge(s_oscale, at)
                    alone(pool, 0)
                    nc.gpsimd.tensor_scalar(shift3[:, col], mv3[:, j, 0:1], factor3[:, col], -1.0, ALU.mult, ALU.mult
                                            ).then_inc(s_oshift, 1)

                def add_tile(j):
                    pool.wait_ge(s_onorm, g * GT + (j + 1))
                    nc.gpsimd.tensor_tensor(fin[:, j, :], fin[:, j, :], x1_now[:, j, :], ALU.add).then_inc(s_fin, 1)

                for j in range(GT):
                    scale_tile(j)
                    if j:
                        add_tile(j - 1)
                add_tile(GT - 1)

            def group(g, first, more):
                for m in range(MC):
                    if first:
                        for n in ternary_in_group(m, 0):
                            less(n)
                    if more and m in CHUNK_SECOND:
                        second_step(g, CHUNK_SECOND[m])
                    if more and m in CHUNK_FIRST:
                        first_factor(g, CHUNK_FIRST[m])
                        first_step(g, CHUNK_FIRST[m])
                finish(g)

            group(0, True, True)
            with pool.Fori(1, G - 1) as g:
                group(g, False, True)
            group(G - 1, False, False)

        @block.scalar
        def _(act):
            def x_hi(n):
                act.wait_ge(s_xt, n + 1)
                nc.scalar.activation(xnt_by_chunk[:, n // QT, 0, :, n % QT * P:(n % QT + 1) * P],
                                     x_bank(n).rearrange("p (c q) -> p c q", c=C),
                                     ACT.Copy).then_inc(s_xhi, 1)

            def proj_hi(h, op, slot, count, bank):
                if op[0] == "V":
                    act.wait_ge(s_proj, count)
                    nc.scalar.activation(v_places(h, op, 0), v_bank(bank), ACT.Copy).then_inc(s_projhi, 1)
                    return
                half = slice(int(op[1]) * HALF, (int(op[1]) + 1) * HALF)
                act.wait_ge(s_proj, count)
                dst = kt[:, slot, 0, half] if op[0] == "K" else qt[:, 0, half]
                nc.scalar.activation(dst, accum[bank][:, :], ACT.Copy, scale=1.0 if op[0] == "K" else SCALE
                                     ).then_inc(s_projhi, 1)

            def split_hi(w, raw_count, proj_count):
                act.wait_ge(s_raw[w[0]], raw_count)
                if proj_count is not None:
                    act.wait_ge(s_proj, proj_count)
                raw, hi, _ = weight_parts(w)
                nc.scalar.activation(hi, raw, ACT.Copy).then_inc(s_split_hi[w[0]], 1)

            pieces = iter(range(PIECES))

            def load_to_weigh(n):
                which, m = (n // MC, n % MC)
                if n >= WEIGH:
                    act.wait_ge(s_abs, n - WEIGH + 1)
                act.dma_start(weigh[:, n % WEIGH, :], (w1, w3, w2)[which][:, m, :]).then_inc(s_weigh[n % WEIGH], 16)

            def weigh_next(count):
                for _, n in zip(range(count), pieces):
                    act.wait_ge(s_weigh[n % WEIGH], 16 * (n // WEIGH + 1))
                    nc.scalar.activation(weigh[:, n % WEIGH, :], weigh[:, n % WEIGH, :], ACT.Abs,
                                         accum_out=abssum[:, n:n + 1]).then_inc(s_abs, 1)
                    if WEIGH <= n + WEIGH - 1 < PIECES and n:
                        load_to_weigh(n + WEIGH - 1)

            for n in range(8):
                x_hi(n)
                if n == 3:
                    for k in range(WEIGH):
                        load_to_weigh(k)
                if n in (2, 4, 6):
                    split_hi(("k", ("v", 0), "q")[n // 2 - 1], 16, None)
            before_first = Head(-1, steps=[])
            split_hi(("v", 1), 32, None)
            for n, op in enumerate(("K0", "K1", "V0", "V1")):
                proj_hi(before_first, op, 0, PROJ[op], n % 2)
                weigh_next(n % 2)
            for n in range(8, 12):
                x_hi(n)
                weigh_next(1)
            split_hi("k", 32, 2)
            weigh_next(1)
            for n, op in enumerate(("Q0", "Q1")):
                proj_hi(before_first, op, 0, PROJ[op], n % 2)
                weigh_next(1)
            for n in range(12, XT):
                x_hi(n)
                weigh_next(1)

            def first_norm(g, j):
                act.wait_ge(s_shift, g * (2 * GT) + (2 * (GT + j) + 1))
                nc.scalar.activation(stage[j % 2][:, 0, :], stage[j % 2][:, 0, :], ACT.Identity, bias=shift[:, 0:1],
                                     scale=rstd[:, 0:1]).then_inc(s_y, 1)

            def second_norm(g, j):
                if isinstance(g, int) and g < 0:
                    act.wait_ge(s_pv, 2 * (NH - 1))
                else:
                    act.wait_ge(s_x1t, g * GT + (j + 1))
                act.wait_ge(s_shift, g * (2 * GT) + (2 * (GT + j) + 2))
                nc.scalar.activation(x1n[:, j, :], x1_next[:, j, :], ACT.Identity, bias=shift[:, 1:2],
                                     scale=rstd[:, 1:2]).then_inc(s_x1n, 1)

            def x1_hi(j, bank, count):
                act.wait_ge(s_x1t, count)
                nc.scalar.activation(x1nt[:, 0, :, j * P:(j + 1) * P], bank.rearrange("p (c q) -> p c q", c=C), ACT.Copy
                                     ).then_inc(s_x1hi, 1)

            for h in heads_of(act):
                for i, step in enumerate(h.steps):
                    if h.n >= NH - 1:
                        k = (h.n - (NH - 1)) * QT + i
                        if k in FIRST_APPLY:
                            first_norm(-1, FIRST_APPLY[k])
                        if k in SECOND_APPLY:
                            second_norm(-1, SECOND_APPLY[k])
                    if "S" in step:
                        act.wait_ge(s_negmax, h.at(QT, i + 1))
                        if i >= 2 or h.n > 0:
                            before = fill(h, i - 2, i - 2 >= 4) if i >= 2 else h.at(FILLS, (-2, 0)[i])
                            act.wait_ge(s_t, before)
                        nc.scalar.activation(probs[:, i % 2, 0:(i + 1) * P], score[i % 2][:, 0:(i + 1) * P], ACT.Exp,
                                             bias=negmax[:, i:i + 1], scale=1.0,
                                             accum_out=rowsum[:, i:i + 1]).then_inc(s_exp, 1)
                    for op in step:
                        if op in PROJ:
                            proj_hi(h, op, h.slot(1), h.at(6, 6 + PROJ[op]), ACC_BANK[op])
                        elif op in ("PV0", "PV1"):
                            half = slice(int(op[2]) * HALF, (int(op[2]) + 1) * HALF)
                            act.wait_ge(s_pv, h.at(2, 1 if op == "PV0" else 0))
                            nc.scalar.activation(zt[:, 0, half], accum[ACC_BANK[op]][:, :], ACT.Copy).then_inc(s_zhi, 1)
                        elif op[0] == "T":
                            q = tile_of(op)
                            if q == 0 and h.n > 0:
                                act.wait_ge(s_pv, h.at(2, 0))
                            if q == 4:
                                act.wait_ge(s_pv, h.at(2, 1))
                            for f, (bank, j0, n) in enumerate(fills_of(op)):
                                act.wait_ge(s_t, h.at(FILLS, FILL[q] + 1 + f - (FILLS if q == 7 else 0)))
                                src = tp[bank][:, 0:n * P].rearrange("p (j q) -> p j q", q=P)
                                for k, (at, m, dst) in enumerate(pt_block(0, q, j0, n)):
                                    ins = nc.scalar.activation(dst, src[:, at:at + m, :], ACT.Copy)
                                ins.then_inc(s_thi, 1)
                        elif op[0] == "X":
                            x1_hi(tile_of(op), tp[tile_of(op) % 2][:, :], tile_of(op) + 1)
                    if "S" in step:
                        for w, _, raw_count, proj_count in splits_at(h, i):
                            split_hi(w, raw_count, proj_count)
                    if h.n == 0:
                        weigh_next(3)

            def group(g, first, more):
                at = lambda per, off: g * per + off
                for m in range(MC):
                    act.wait_ge(s_h, at(MC, m + 1))
                    nc.scalar.activation(gate, score[m % 2][:, 0:HALF], ACT.Silu, scale=scales[:, 0:1]).then_inc(s_silu, 1)
                    act.wait_ge(s_gated, at(MC, m + 1))
                    nc.scalar.activation(gt[0][m], ghid, ACT.Copy).then_inc(s_ghi, 1)
                    if more and m - 1 in CHUNK_SECOND:
                        second_norm(g, CHUNK_SECOND[m - 1])
                    if more and m - 1 in CHUNK_FIRST:
                        first_norm(g, CHUNK_FIRST[m - 1])
                    if m == 1 and not first:
                        for j in range(GT):
                            act.wait_ge(s_fin, at(GT, j + 1 - GT))
                            act.dma_start(out[bass.ds(g * HALF + (j * P - HALF), P), :], fin[:, j, :]
                                          ).then_inc(s_out, 16)
                    if m == 0:
                        act.wait_ge(s_x1n, at(GT, GT))
                        if not first:
                            act.wait_ge(s_fin, at(GT, 0))
                        nc.scalar.activation(x1_now, x1_next, ACT.Copy).then_inc(s_now, 1)

                def normalise(j):
                    act.wait_ge(s_oshift, at(GT, j + 1))
                    if first:
                        act.wait_ge(s_part, 32 * QUADS)
                    else:
                        act.wait_ge(s_out, at(GT * 16, 0))
                    nc.scalar.activation(fin[:, j, :], ff_bank(j), ACT.Identity, bias=shift3[:, j:j + 1],
                                         scale=factor3[:, j:j + 1]).then_inc(s_onorm, 1)

                for j in range(GT):
                    if more and j < 2:
                        for k in (2 * j, 2 * j + 1):
                            x1_hi(k, x1_bank(k), at(GT, GT + k + 1))
                    normalise(j)

            group(0, True, True)
            with act.Fori(1, G - 1) as g:
                group(g, False, True)
            group(G - 1, False, False)

        @block.vector
        def _(dve):
            nc.vector.memset(f32(pt[:, :, QT - 1, 2 * P:3 * P]), 0.0).then_inc(s_ptzero, 1)
            dve.sem_inc(s_sum, QT)

            def x_stats(n):
                k = n % NX
                dve.wait_ge(s_xin[k], 16 * (n // NX + 1))
                nc.vector.bn_stats(stats_x[:, k, :], xin[n % NX]).then_inc(s_bn, 1)
                dve.wait_ge(s_bn, n + 1)
                nc.vector.bn_aggr(mv_x[:, k, :], stats_x[:, k, :]).then_inc(s_var, 1)

            def x_norm(n):
                dve.wait_ge(s_rstd, n // 2 + 1)
                k = n % NX
                nc.vector.tensor_scalar(xin[k], xin[k], mv_x[:, k, 0:1], rstd_x[:, k:k + 1], ALU.subtract, ALU.mult
                                        ).then_inc(s_xn[0], 1)

            def x_lo(n):
                dve.wait_ge(s_xhi, n + 1)
                cols = slice(n % QT * P, (n % QT + 1) * P)
                nc.vector.tensor_tensor(xnt_by_chunk[:, n // QT, 1, :, cols],
                                        x_bank(n).rearrange("p (c q) -> p c q", c=C),
                                        f32(xnt_by_chunk[:, n // QT, 0, :, cols]), ALU.subtract).then_inc(s_xlo, 1)

            def proj_lo(h, op, slot, count, bank):
                half = slice(int(op[1]) * HALF, (int(op[1]) + 1) * HALF)
                dve.wait_ge(s_projhi, count)
                if op[0] == "V":
                    nc.vector.tensor_tensor(v_places(h, op, 1), v_bank(bank), f32(v_places(h, op, 0)), ALU.subtract
                                            ).then_inc(s_projlo, 1)
                elif op[0] == "K":
                    nc.vector.tensor_tensor(kt[:, slot, 1, half], accum[bank][:, :], f32(kt[:, slot, 0, half]),
                                            ALU.subtract).then_inc(s_projlo, 1)
                else:
                    nc.vector.scalar_tensor_tensor(qt[:, 1, half], accum[bank][:, :], SCALE, f32(qt[:, 0, half]),
                                                   ALU.mult, ALU.subtract).then_inc(s_projlo, 1)

            before_first = Head(-1, steps=[])
            for n in range(4):
                x_stats(n)
            for n in range(0, 8, 2):
                x_norm(n)
                if n < 4:
                    x_stats(n + 4)
                    x_stats(n + 5)
                if n:
                    x_lo(n - 2)
                    x_lo(n - 1)
            x_lo(6)
            x_lo(7)
            for n in range(8, 12):
                x_stats(n)
            for n, op in enumerate(("K0", "K1", "V0", "V1")):
                proj_lo(before_first, op, 0, PROJ[op], n % 2)
                x_norm(8 + 2 * n)
                if n < 2:
                    x_stats(12 + 2 * n)
                    x_stats(13 + 2 * n)
            for n in range(8, 12):
                x_lo(n)
            for n, op in enumerate(("Q0", "Q1")):
                proj_lo(before_first, op, 0, PROJ[op], n % 2)
            for n in range(12, XT):
                x_lo(n)

            def add_out(h, i):
                dve.wait_ge(s_o, h.at(QT, i + 1 - QT))
                if (h.n - 1) % BODY == 0 and i == 0:
                    dve.wait_ge(s_accfree, h.turn + 1 if h.turn is not None else (h.n - 1) // BODY + 1)
                if h.turn is not None and h.n == 1:
                    nc.vector.scalar_tensor_tensor(acc[:, i, :], acc[:, i, :], keep[:, bass.ds(h.turn, 1)],
                                                   accum[ACC_BANK[f"O{i}"]][:, :], ALU.mult, ALU.add).then_inc(s_sum, 1)
                else:
                    nc.vector.tensor_tensor(acc[:, i, :], accum[ACC_BANK[f"O{i}"]][:, :], acc[:, i, :], ALU.add
                                            ).then_inc(s_sum, 1)

            def ternary(n):
                dve.wait_ge(s_less, n + 1)
                w = weight_of(n)[0]
                slot = piece_slot(n)
                nc.vector.scalar_tensor_tensor(ternary_place(n), wraw[slot], above[:, w:w + 1], is_less[slot],
                                               ALU.is_gt, ALU.subtract).then_inc(s_tern, 1)

            def statistics(k, src, count):
                nc.vector.bn_stats(stats[:, k, :], src).then_inc(s_fbn, 1)
                dve.wait_ge(s_fbn, count)
                alone(dve, 1)
                nc.vector.bn_aggr(mv[:, k, :], stats[:, k, :]).then_inc(s_fvar, 1)

            def first_stats(g, j):
                dve.wait_ge(s_stage[j % 2], g * 64 + (64 + 32 + 32 * (j // 2)))
                statistics(0, stage[j % 2][:, 0, :], g * (2 * GT) + (2 * (GT + j) + 1))

            def second_stats(g, j):
                dve.wait_ge(s_x1, g * GT + (GT + j + 1))
                if j or not isinstance(g, int) or g >= 0:
                    dve.wait_ge(s_x1n, g * GT + (GT + j))
                statistics(1, x1_next[:, j, :], g * (2 * GT) + (2 * (GT + j) + 2))

            def x1_lo(j, bank, count):
                dve.wait_ge(s_x1hi, count)
                cols = slice(j * P, (j + 1) * P)
                nc.vector.tensor_tensor(x1nt[:, 1, :, cols], bank.rearrange("p (c q) -> p c q", c=C),
                                        f32(x1nt[:, 0, :, cols]), ALU.subtract).then_inc(s_x1lo, 1)

            for h in heads_of(dve):
                for i, step in enumerate(h.steps):
                    if "S" in step:
                        dve.wait_ge(s_score, h.at(QT, i + 1))
                        nc.vector.tensor_reduce(negmax[:, i:i + 1], score[i % 2][:, 0:(i + 1) * P], AX.X, ALU.max,
                                                negate=True).then_inc(s_negmax, 1)
                    if i > 0 and "O" in h.steps[i - 1] and h.n < NH - 1:
                        add_out(h, i - 1)
                    if "S" in step:
                        dve.wait_ge(s_exp, h.at(QT, i + 1))
                        nc.vector.reciprocal(rinv[:, i:i + 1], rowsum[:, i:i + 1]).then_inc(s_rinv, 1)
                    for op in step:
                        if op in PROJ:
                            proj_lo(h, op, h.slot(1), h.at(6, 6 + PROJ[op]), ACC_BANK[op])
                        elif op in ("PV0", "PV1"):
                            half = slice(int(op[2]) * HALF, (int(op[2]) + 1) * HALF)
                            dve.wait_ge(s_zhi, h.at(2, 1 if op == "PV0" else 0))
                            nc.vector.tensor_tensor(zt[:, 1, half], accum[ACC_BANK[op]][:, :], f32(zt[:, 0, half]),
                                                    ALU.subtract).then_inc(s_zlo, 1)
                        elif op[0] == "T":
                            q = tile_of(op)
                            for f, (bank, j0, n) in enumerate(fills_of(op)):
                                dve.wait_ge(s_thi, h.at(FILLS, FILL[q] + 1 + f - (FILLS if q == 7 else 0)))
                                src = tp[bank][:, 0:n * P].rearrange("p (j q) -> p j q", q=P)
                                for (at, m, hi), (_, _, lo) in zip(pt_block(0, q, j0, n), pt_block(1, q, j0, n)):
                                    ins = nc.vector.tensor_tensor(lo, src[:, at:at + m, :], f32(hi), ALU.subtract)
                                ins.then_inc(s_tlo, 1)
                        elif op[0] == "X":
                            x1_lo(tile_of(op), tp[tile_of(op) % 2][:, :], tile_of(op) + 1)
                        elif op == "M":
                            dve.wait_ge(s_mean, 1)
                            for dst, k in ((scales, 1.0), (above, 0.5), (below, -0.5)):
                                nc.vector.tensor_scalar(dst, accum[0][:, 0:3], k / (HIDDEN * D), None, ALU.mult
                                                        ).then_inc(s_thr, 1)
                            dve.wait_ge(s_thr, 3)
                            nc.vector.tensor_tensor(squared, scales[:, 2:3], scales[:, 2:3], ALU.mult).then_inc(s_thr, 1)
                    if h.n >= NH - 1:
                        add_out(h, i)
                    if h.turn is None and h.n >= TERNARY:
                        for n in ternary_in_head(h.n, i, 1):
                            ternary(n)
                    if h.n >= NH - 1:
                        k = (h.n - (NH - 1)) * QT + i
                        if k in SECOND_STATS:
                            second_stats(-1, SECOND_STATS[k])
                        if k in FIRST_STATS:
                            first_stats(-1, FIRST_STATS[k])
                if "O" in h.steps[QT - 1] and h.n < NH - 1:
                    add_out(h, QT - 1)
                if h.n == 0:
                    dve.wait_ge(s_abs, PIECES)
                    nc.vector.tensor_reduce(totals, abssum.rearrange("p (w m) -> p w m", w=3), AX.X, ALU.add
                                            ).then_inc(s_tot, 1)
                    dve.wait_ge(s_acczero, 1)
                    dve.wait_ge(s_const, 4)

            def group(g, first, more):
                at = lambda per, off: g * per + off
                for m in range(MC):
                    dve.wait_ge(s_silu, at(MC, m + 1))
                    if m == 0 and first:
                        dve.wait_ge(s_raw["v"], 16 * (NH + 1))
                    if m or not first:
                        dve.wait_ge(s_glo, at(MC, m))
                    nc.vector.scalar_tensor_tensor(ghid, score[m % 2][:, HALF:2 * HALF], scales[:, 1:2], gate,
                                                   ALU.mult, ALU.mult).then_inc(s_gated, 1)
                    if first:
                        for n in ternary_in_group(m, 1):
                            ternary(n)
                    if more and m in CHUNK_SECOND:
                        second_stats(g, CHUNK_SECOND[m])
                    if more and m in CHUNK_FIRST:
                        first_stats(g, CHUNK_FIRST[m])
                    dve.wait_ge(s_ghi, at(MC, m + 1))
                    nc.vector.tensor_tensor(gt[1][m], ghid, f32(gt[0][m]), ALU.subtract).then_inc(s_glo, 1)
                for j in range(GT):
                    if more and j < 2:
                        for k in (2 * j, 2 * j + 1):
                            x1_lo(k, x1_bank(k), at(GT, GT + k + 1))
                    dve.wait_ge(s_f, at(GT, j + 1))
                    nc.vector.bn_stats(stats3[:, j, :], ff_bank(j)).then_inc(s_obn, 1)
                    dve.wait_ge(s_obn, at(GT, j + 1))
                    alone(dve, 1)
                    nc.vector.bn_aggr(mv3[:, j, :], stats3[:, j, :]).then_inc(s_ovar, 1)

            group(0, True, True)
            with dve.Fori(1, G - 1) as g:
                group(g, False, True)
            group(G - 1, False, False)

        @block.tensor
        def _(pe):
            pe.wait_ge(s_const, 4)

            def x_transpose(n, free):
                pe.wait_ge(s_xn[n % 2], n // 2 + 1)
                if free:
                    pe.wait_ge(*free)
                for c in range(C):
                    ins = nc.tensor.transpose(x_bank(n)[:, c * P:(c + 1) * P], xin[n % NX][:, c * P:(c + 1) * P],
                                              identity[:, :])
                ins.then_inc(s_xt, 1)

            def project(h, op, bank):
                batch = h.next_batch
                if op[0] == "V":
                    for t in range(2):
                        tile = (0 if h.n % 2 else QT // 2) + 2 * int(op[1]) + t
                        for c in range(C):
                            for k, (a, b) in enumerate(((0, 0), (0, 1), (1, 0))):
                                ins = nc.tensor.matmul(accum[bank][:, t * 2 * E:(t + 1) * 2 * E],
                                                       xnt_flat[:, x_columns(batch, a, c, tile * P, P)],
                                                       w_v[:, b, c, :], start=(c == 0 and k == 0),
                                                       stop=(c == C - 1 and k == 2))
                    ins.then_inc(s_proj, 1)
                    return
                first = int(op[1]) * HALF
                w = {"K": w_k, "Q": w_q}[op[0]]
                for c in range(C):
                    for k, (a, b) in enumerate(((0, 0), (0, 1), (1, 0))):
                        ins = nc.tensor.matmul(accum[bank][:, :], w[:, a, c, :],
                                               xnt_flat[:, x_columns(batch, b, c, first, HALF)],
                                               start=(c == 0 and k == 0), stop=(c == C - 1 and k == 2))
                ins.then_inc(s_proj, 1)

            before_first = Head(-1, steps=[])
            for n in range(6):
                x_transpose(n, (s_xlo, n - 3) if n >= 4 else None)
            for n, op in enumerate(("K0", "K1", "V0", "V1")):
                pe.wait_ge(s_xlo, 8 if n else 4)
                pe.wait_ge(s_split[op[0].lower()], 2 if op[0] == "V" else 1)
                if n >= 2:
                    pe.wait_ge(s_projlo, n - 1)
                project(before_first, op, n % 2)
                if n == 0:
                    for k in (6, 7):
                        x_transpose(k, (s_xlo, k - 3))
            for n in range(8, 12):
                x_transpose(n, (s_xlo, n - 3))
            for n, op in enumerate(("Q0", "Q1")):
                pe.wait_ge(s_split["q"], 1)
                pe.wait_ge(s_projlo, 3 + n)
                project(before_first, op, n)
            for n in range(12, XT):
                x_transpose(n, (s_xlo, n - 3))

            def acc_free(h, op):
                was = h.before[op]
                back = was.endswith("-")
                was = was.rstrip("-")
                if was == "M":
                    pe.wait_ge(s_thr, 3)
                elif was in PROJ:
                    pe.wait_ge(s_projlo, h.at(6, PROJ[was] + (0 if back else 6)))
                elif was == "PV0":
                    pe.wait_ge(s_zlo, h.at(2, 1 - 2 * back))
                elif was == "PV1":
                    pe.wait_ge(s_zlo, h.at(2, 0))
                else:
                    pe.wait_ge(s_sum, h.at(QT, tile_of(was) + 1 - QT * back))

            def tp_free(h, op, bank):
                if h.n == 0 and op in ("T0", "T1"):
                    pe.wait_ge(s_xlo, XT)
                    return
                was, _ = TP_BEFORE[op, bank]
                q = int(was[1])
                previous = q == 7 or was.endswith("-")
                pe.wait_ge(s_tlo, h.at(FILLS, FILL[q] + 1 + (bank == 1 and q >= 4) - FILLS * previous))

            def scores(h, i):
                if i == 0:
                    pe.wait_ge(s_projlo, h.at(6, PROJ["Q0"]))
                if i == 4:
                    pe.wait_ge(s_projlo, h.at(6, PROJ["Q1"]))
                if i == 1 and h.n == 0:
                    pe.wait_ge(s_xlo, XT)
                if i >= 2 or h.n > 0:
                    pe.wait_ge(s_exp, h.at(QT, i - 1))
                dst, slot = score[i % 2], h.slot(0)
                q = slice(i * P, (i + 1) * P)
                banks = [(0, WIDTH[i])] if i < 4 else [(0, HALF), (HALF, HALF + WIDTH[i - 4])]
                for b, (k0, k1) in enumerate(banks):
                    for n, (a, c) in enumerate(((0, 0), (0, 1), (1, 0))):
                        nc.tensor.matmul(dst[:, k0:k1], qt[:, a, q], kt[:, slot, c, k0:k1],
                                         start=(n == 0), stop=(n == 2 and b < i // 4))
                nc.tensor.matmul(dst[:, i * P:(i + 1) * P], identity_b[:, :], mask[:, :], start=False, stop=True
                                 ).then_inc(s_score, 1)

            def p_transpose(h, op):
                q = tile_of(op)
                pe.wait_ge(s_norm, h.at(QT, q + 1 - (QT if q == 7 else 0)))
                for bank, j0, n in fills_of(op):
                    tp_free(h, op, bank)
                    for j in range(n):
                        ins = nc.tensor.transpose(tp[bank][:, j * P:(j + 1) * P],
                                                  probs[:, q % 2, (j0 + j) * P:(j0 + j + 1) * P], identity[:, :])
                    ins.then_inc(s_t, 1)

            def values(h, op):
                group = int(op[2])
                low, high = v_slot(h, group), h.slot(-1 if group else 0)
                back = FILLS if group else 0
                pe.wait_ge(s_tlo, h.at(FILLS, (FILL[7] + 2 if group else FILL[3] + 1) - back))
                dst = accum[ACC_BANK[op]]
                tiles = 4 * group + 4
                for j in range(tiles):
                    first = max(0, j - 4 * group)
                    q = slice(min(first, 2) * P, HALF)
                    values_of = v_low[:, low] if j < 4 else v_high[:, high]
                    for n, (a, b) in enumerate(((0, 0), (0, 1), (1, 0))):
                        ins = nc.tensor.matmul(dst[:, q], values_of[:, a, j % 4 * P:(j % 4 + 1) * P],
                                               pt[:, b, key_slot(group, j), q],
                                               start=(j == 0 and n == 0), stop=(j == tiles - 1 and n == 2))
                ins.then_inc(s_pv, 1)

            def output(h, i):
                slot = h.slot(-1)
                if i == 0:
                    pe.wait_ge(s_split["o"], h.at(1, 0))
                    pe.wait_ge(s_zlo, h.at(2, -1))
                if i == 4:
                    pe.wait_ge(s_zlo, h.at(2, 0))
                for n, (a, b) in enumerate(((0, 0), (0, 1), (1, 0))):
                    ins = nc.tensor.matmul(accum[ACC_BANK[f"O{i}"]][:, :], zt[:, a, i * P:(i + 1) * P],
                                           w_o[:, slot, b, :], start=(n == 0), stop=(n == 2))
                ins.then_inc(s_o, 1)

            def x1_transpose(j, count, bank, free):
                pe.wait_ge(s_x1n, count)
                pe.wait_ge(*free)
                for c in range(C):
                    ins = nc.tensor.transpose(bank[:, c * P:(c + 1) * P], x1n[:, j, c * P:(c + 1) * P], identity[:, :])
                ins.then_inc(s_x1t, 1)

            pe.wait_ge(s_ptzero, 1)
            for h in heads_of(pe):
                for i, step in enumerate(h.steps):
                    for op in step:
                        if op == "S":
                            scores(h, i)
                        elif op in PROJ:
                            pe.wait_ge(s_split[op[0].lower()], h.at(1, 3 if op[0] == "V" and h.n % 2 else 2))
                            acc_free(h, op)
                            project(h, op, ACC_BANK[op])
                        elif op in ("PV0", "PV1"):
                            acc_free(h, op)
                            values(h, op)
                        elif op == "O":
                            acc_free(h, f"O{i}")
                            output(h, i)
                        elif op == "M":
                            acc_free(h, op)
                            pe.wait_ge(s_tot, 1)
                            nc.tensor.matmul(accum[0][:, 0:3], ones[:, :], totals, start=True, stop=True
                                             ).then_inc(s_mean, 1)
                        elif op[0] == "X":
                            j = tile_of(op)
                            free = (s_tlo, h.at(FILLS, FILL[7] + 1 + j - FILLS)) if j < 2 else (s_x1lo, j - 1)
                            x1_transpose(j, j + 1, tp[j % 2][:, :], free)
                        else:
                            p_transpose(h, op)

            def group(g, first, more):
                at = lambda per, off: g * per + off
                for m in range(MC):
                    if first:
                        pe.wait_ge(s_tern, 2 * m + 2)
                    if m < 2:
                        pe.wait_ge(s_x1lo, at(GT, 4))
                    else:
                        pe.wait_ge(s_gated, at(MC, m - 1))
                    for w in range(2):
                        for c in range(C):
                            for b in range(2):
                                ins = nc.tensor.matmul(score[m % 2][:, w * HALF:(w + 1) * HALF], w13t[:, m, w, c, :],
                                                       x1nt[:, b, c, :], start=(c == 0 and b == 0),
                                                       stop=(c == C - 1 and b == 1))
                    ins.then_inc(s_h, 1)
                for j in range(GT):
                    if not first:
                        pe.wait_ge(s_onorm, at(GT, j + 1 - GT))
                    elif j == 0:
                        pe.wait_ge(s_sum, QT + QT * NH)
                    for m in range(MC):
                        if j == 0:
                            pe.wait_ge(s_glo, at(MC, m + 1))
                            if first:
                                pe.wait_ge(s_tern, 2 * MC + m + 1)
                        for a in range(2):
                            ins = nc.tensor.matmul(ff_bank(j), gt[a][m][:, j * P:(j + 1) * P], w2t[:, m, :],
                                                   start=(m == 0 and a == 0), stop=(m == MC - 1 and a == 1))
                    ins.then_inc(s_f, 1)
                    if more and j < 2:
                        for k in (2 * j, 2 * j + 1):
                            x1_transpose(k, at(GT, GT + k + 1), x1_bank(k), (s_gated, at(MC, MC - 1 + j)))

            group(0, True, True)
            with pe.Fori(1, G - 1) as g:
                group(g, False, True)
            group(G - 1, False, False)


def kernel(**inputs):
    import numpy as np
    import concourse.bacc as bacc
    from concourse.bass_utils import run_bass_kernel_spmd

    a = {k: np.asarray(val) for k, val in inputs.items()}

    def by_model_dim(w):
        return np.ascontiguousarray(w.reshape(HEADS, E, C, P).transpose(0, 3, 2, 1)).reshape(HEADS, P, C * E)

    def ffn_in(w):
        w = np.pad(w, ((0, MC * P - HIDDEN), (0, 0))).reshape(MC, P, C, P)
        return np.ascontiguousarray(w.transpose(3, 0, 2, 1)).reshape(P, MC, C * P)

    w2 = np.pad(a["L0_ffn_w2"].T, ((0, MC * P - HIDDEN), (0, 0))).reshape(MC, P, D)
    arrays = {
        "x": np.ascontiguousarray(a["L0_attn_x"].reshape(TOK, D)),
        "wq": by_model_dim(a["L0_attn_W_Q"]),
        "wk": by_model_dim(a["L0_attn_W_K"]),
        "wv": by_model_dim(a["L0_attn_W_V"]),
        "wo": np.ascontiguousarray(a["L0_attn_W_O"].transpose(0, 2, 1)),
        "w1": ffn_in(a["L0_ffn_w1"]),
        "w3": ffn_in(a["L0_ffn_w3"]),
        "w2": np.ascontiguousarray(w2.transpose(1, 0, 2)),
    }
    nc = bacc.Bacc("TRN2", target_bir_lowering=False, num_devices=1, dynamic_dma_scratch_size=4096)
    args = [nc.dram_tensor(name, val.shape, mybir.dt.from_np(val.dtype), kind="ExternalInput").ap()
            for name, val in arrays.items()]
    out = nc.dram_tensor("out", [TOK, D], F32, kind="ExternalOutput").ap()
    block_kernel(nc, *args, out)
    r = run_bass_kernel_spmd(nc, [arrays], core_ids=[0])
    return r.results[0]["out"].reshape(BATCH, SEQ, D)
```
